# Optimizing a Trainium2 kernel written in Bass

```python
import numpy as np
import jax
import jax.numpy as jnp

def _softmax(x, axis=-1):
    return jax.nn.softmax(x, axis=axis)

def _gelu(x):
    return jax.nn.gelu(x, approximate=True)

def _silu(x):
    return jax.nn.silu(x)

def _sigmoid(x):
    return jax.nn.sigmoid(x)

def _layernorm(x, axis=-1, eps=1e-05):
    m = jnp.mean(x, axis=axis, keepdims=True)
    v = jnp.var(x, axis=axis, keepdims=True)
    return (x - m) / jnp.sqrt(v + eps)

def _scatter_add(tgt, idx, src, axis=0):
    return tgt.at[idx].add(src)

def _segment_sum(src, seg, n):
    return jax.ops.segment_sum(src, seg, n)
kernel_name = 'mk_decoder_preln_d1_seqx_r8_f82404'

def setup_inputs(seed: int=0):
    np.random.seed(seed)
    _w = jnp.asarray

    def _rec_inputs():
        import jax
        import jax.numpy as jnp
        _rk = jax.random.key(seed)
        x = 7.22e-05 + 1 * jax.random.normal(jax.random.fold_in(_rk, 1), (16, 64, 256), jnp.float32)
        _lenS = 64 - jax.random.randint(jax.random.fold_in(_rk, 7), (16,), 0, max(1, 64 // 4) + 1, jnp.int32)
        _lenS2 = 64 - jax.random.randint(jax.random.fold_in(_rk, 8), (16,), 0, max(1, 64 // 4) + 1, jnp.int32)
        _ctx_2048P = jax.random.normal(jax.random.fold_in(_rk, 11), (16, 16, 256), jnp.float32)
        _ctx_2048c = jax.random.dirichlet(jax.random.fold_in(_rk, 511), 0.3 * jnp.ones((16,), jnp.float32), (16, 64))
        _ctx_2048t = jnp.einsum('bsk,bkd->bsd', _ctx_2048c, _ctx_2048P)
        _ctx_2048t = _ctx_2048t * jax.lax.rsqrt(jnp.mean(jnp.square(_ctx_2048t)) + 1e-12) * 0.953939
        ctx_2048 = 4.13588e-05 + 0.999923 * (_ctx_2048t + 0.3 * jax.random.normal(jax.random.fold_in(_rk, 611), (16, 64, 256), jnp.float32))
        return (x, ctx_2048)
    x, ctx_2048 = _rec_inputs()

    def _L0_attn_setup():
        import jax, jax.numpy as jnp
        import numpy as np
        N_KV_HEAD = 8
        GROUP_SIZE = 4
        ROPE_BASE = 10000.0

        def _rope(x):
            t, d = (x.shape[-2], x.shape[-1])
            j = jnp.arange(d // 2, dtype=jnp.float32)
            theta = jnp.asarray(ROPE_BASE, jnp.float32) ** (-2.0 * j / d)
            pos = (jnp.arange(t, dtype=jnp.float32) + 1.0)[:, None]
            ang = pos * theta[None, :]
            C = jnp.concatenate([ang, ang], axis=-1)
            x2 = jnp.concatenate([-x[..., d // 2:], x[..., :d // 2]], axis=-1)
            return x * jnp.cos(C) + x2 * jnp.sin(C)
        key = jax.random.key(seed)
        ks = jax.random.split(key, 9)
        b, t, e = (2, 256, 256)
        kv = e // GROUP_SIZE
        s_in = 1.0 / np.sqrt(e)
        return {'x': jax.random.normal(ks[0], (b, t, e), jnp.float32), 'Wq': jax.random.normal(ks[1], (e, e), jnp.float32) * s_in, 'bq': jax.random.normal(ks[2], (e,), jnp.float32) * 0.01, 'Wk': jax.random.normal(ks[3], (kv, e), jnp.float32) * s_in, 'bk': jax.random.normal(ks[4], (kv,), jnp.float32) * 0.01, 'Wv': jax.random.normal(ks[5], (kv, e), jnp.float32) * s_in, 'bv': jax.random.normal(ks[6], (kv,), jnp.float32) * 0.01, 'Wo': jax.random.normal(ks[7], (e, e), jnp.float32) * s_in, 'bo': jax.random.normal(ks[8], (e,), jnp.float32) * 0.01}
    _L0_attn_all = _L0_attn_setup()
    _L0_attn_in = {k: v for k, v in _L0_attn_all.items() if k in ('Wq', 'bq', 'Wk', 'bk', 'Wv', 'bv', 'Wo', 'bo')}
    del _L0_attn_all

    def _L0_xattn_setup():
        import jax, jax.numpy as jnp
        import numpy as np
        N_HEAD = 8
        key = jax.random.key(seed)
        k1, k2, k3 = jax.random.split(key, 3)
        B, D, L = (4, 128, 256)
        q = jax.random.normal(k1, (B, D, L), dtype=jnp.float32)
        k = jax.random.normal(k2, (B, D, L), dtype=jnp.float32)
        v = jax.random.normal(k3, (B, D, L), dtype=jnp.float32)
        gamma = jnp.ones((), dtype=jnp.float32)
        return {'q': q, 'k': k, 'v': v, 'gamma': gamma}
    _L0_xattn_all = _L0_xattn_setup()
    _L0_xattn_in = {k: v for k, v in _L0_xattn_all.items() if k in ('gamma',)}
    del _L0_xattn_all

    def _L0_ffn_setup():
        import jax, jax.numpy as jnp
        import numpy as np
        FP8_MAX = 448.0

        def _fp8_matmul(x2d, w):
            scale_x = jnp.maximum(jnp.max(jnp.abs(x2d)) / FP8_MAX, 1e-06)
            scale_w = jnp.maximum(jnp.max(jnp.abs(w)) / FP8_MAX, 1e-06)
            x8 = (x2d / scale_x).astype(jnp.float8_e4m3fn)
            w8 = (w / scale_w).astype(jnp.float8_e4m3fn)
            out = jnp.matmul(x8.astype(x2d.dtype), w8.astype(x2d.dtype).T)
            return out * (scale_x * scale_w)
        key = jax.random.key(seed)
        k1, k2, k3 = jax.random.split(key, 3)
        dim = 256
        B, S = (4, 256)
        x = jax.random.normal(k1, (B, S, dim), dtype=jnp.float32)
        std = 0.5 * dim ** (-0.5)
        w_fc = jax.random.normal(k2, (4 * dim, dim), dtype=jnp.float32) * std
        w_proj = jax.random.normal(k3, (dim, 4 * dim), dtype=jnp.float32) * std
        return {'x': x, 'w_fc': w_fc, 'w_proj': w_proj}
    _L0_ffn_all = _L0_ffn_setup()
    _L0_ffn_in = {k: v for k, v in _L0_ffn_all.items() if k in ('w_fc', 'w_proj')}
    del _L0_ffn_all
    return {'x': x, 'ctx_2048': ctx_2048, 'L0_attn_Wq': _L0_attn_in['Wq'], 'L0_attn_bq': _L0_attn_in['bq'], 'L0_attn_Wk': _L0_attn_in['Wk'], 'L0_attn_bk': _L0_attn_in['bk'], 'L0_attn_Wv': _L0_attn_in['Wv'], 'L0_attn_bv': _L0_attn_in['bv'], 'L0_attn_Wo': _L0_attn_in['Wo'], 'L0_attn_bo': _L0_attn_in['bo'], 'L0_xattn_gamma': _L0_xattn_in['gamma'], 'L0_ffn_w_fc': _L0_ffn_in['w_fc'], 'L0_ffn_w_proj': _L0_ffn_in['w_proj']}

def reference(x, ctx_2048, L0_attn_Wq, L0_attn_bq, L0_attn_Wk, L0_attn_bk, L0_attn_Wv, L0_attn_bv, L0_attn_Wo, L0_attn_bo, L0_xattn_gamma, L0_ffn_w_fc, L0_ffn_w_proj):
    import jax
    import jax.numpy as jnp

    def _L0_attn_ref(x, Wq, bq, Wk, bk, Wv, bv, Wo, bo):
        import jax, jax.numpy as jnp
        import numpy as np
        N_KV_HEAD = 8
        GROUP_SIZE = 4
        ROPE_BASE = 10000.0

        def _rope(x):
            t, d = (x.shape[-2], x.shape[-1])
            j = jnp.arange(d // 2, dtype=jnp.float32)
            theta = jnp.asarray(ROPE_BASE, jnp.float32) ** (-2.0 * j / d)
            pos = (jnp.arange(t, dtype=jnp.float32) + 1.0)[:, None]
            ang = pos * theta[None, :]
            C = jnp.concatenate([ang, ang], axis=-1)
            x2 = jnp.concatenate([-x[..., d // 2:], x[..., :d // 2]], axis=-1)
            return x * jnp.cos(C) + x2 * jnp.sin(C)
        b, t, e = x.shape
        h, g = (N_KV_HEAD, GROUP_SIZE)
        d = e // (h * g)
        q = x @ Wq.T + bq
        k = x @ Wk.T + bk
        v = x @ Wv.T + bv
        q = q.reshape(b, t, h, g, d).transpose(0, 3, 2, 1, 4)
        k = k.reshape(b, t, h, d).transpose(0, 2, 1, 3)
        v = v.reshape(b, t, h, d).transpose(0, 2, 1, 3)
        q = _rope(q)
        k = _rope(k)
        scale = jnp.asarray(np.sqrt(d), x.dtype)
        att = jnp.einsum('bghqd,bhkd->bghqk', q, k) / scale
        causal = jnp.tril(jnp.ones((t, t), bool))
        att = jnp.where(causal, att, -jnp.inf)
        att = jax.nn.softmax(att, axis=-1)
        y = jnp.einsum('bghqk,bhkd->bghqd', att, v)
        y = y.transpose(0, 3, 2, 1, 4).reshape(b, t, e)
        return y @ Wo.T + bo

    def _L0_xattn_ref(q, k, v, gamma):
        import jax, jax.numpy as jnp
        import numpy as np
        N_HEAD = 8
        B, Dq, Lq = q.shape
        Dv, Lk = (v.shape[-2], v.shape[-1])
        h = N_HEAD
        dq = Dq // h
        dv = Dv // h
        qh = q.reshape(B, h, dq, Lq)
        kh = k.reshape(B, h, dq, Lk)
        vh = v.reshape(B, h, dv, Lk)
        scale = 1.0 / jnp.sqrt(jnp.asarray(dq, dtype=q.dtype))
        qk = jnp.einsum('bhdq,bhdl->bhql', qh, kh) * scale
        sm = jax.nn.softmax(qk, axis=-1)
        ret = jnp.einsum('bhql,bhdl->bhdq', sm, vh)
        ret = ret.reshape(B, Dv, Lq)
        return gamma * ret

    def _L0_ffn_ref(x, w_fc, w_proj):
        import jax, jax.numpy as jnp
        import numpy as np
        FP8_MAX = 448.0

        def _fp8_matmul(x2d, w):
            scale_x = jnp.maximum(jnp.max(jnp.abs(x2d)) / FP8_MAX, 1e-06)
            scale_w = jnp.maximum(jnp.max(jnp.abs(w)) / FP8_MAX, 1e-06)
            x8 = (x2d / scale_x).astype(jnp.float8_e4m3fn)
            w8 = (w / scale_w).astype(jnp.float8_e4m3fn)
            out = jnp.matmul(x8.astype(x2d.dtype), w8.astype(x2d.dtype).T)
            return out * (scale_x * scale_w)
        shape = x.shape
        x2d = x.reshape(-1, shape[-1])
        h = _fp8_matmul(x2d, w_fc)
        h = jnp.square(jax.nn.relu(h))
        out = _fp8_matmul(h, w_proj)
        return out.reshape(*shape[:-1], -1)
    x = x + _L0_attn_ref(_layernorm(x, axis=-1), L0_attn_Wq, L0_attn_bq, L0_attn_Wk, L0_attn_bk, L0_attn_Wv, L0_attn_bv, L0_attn_Wo, L0_attn_bo)
    x = x + _L0_xattn_ref(_layernorm(x, axis=-1), ctx_2048, ctx_2048, L0_xattn_gamma)
    x = x + _L0_ffn_ref(_layernorm(x, axis=-1), L0_ffn_w_fc, L0_ffn_w_proj)
    return x

_drawn_inputs = setup_inputs


def setup_inputs(seed=0):
    import zlib

    import numpy as np

    out = dict(_drawn_inputs(seed))
    spreads = {}
    factors = {'L0_attn_bq': 20.693, 'L0_attn_bk': 29.467, 'L0_attn_bv': 3.598, 'L0_attn_bo': 3.773}
    for name, (base, spread) in spreads.items():
        noise = np.random.default_rng([zlib.crc32(name.encode()), seed]).standard_normal(out[name].shape)
        drawn = base * np.exp(spread * noise) if base else spread * noise
        out[name] = jnp.asarray(drawn.astype(out[name].dtype))
    for name, factor in factors.items():
        out[name] = (out[name] * factor).astype(out[name].dtype)
    return out
```

```python
from contextlib import ExitStack

import concourse.bass as bass
from concourse import mybir

ALU = mybir.AluOpType
ACT = mybir.ActivationFunctionType
AX = mybir.AxisListType
F32 = mybir.dt.float32
BF16 = mybir.dt.bfloat16
FP8 = mybir.dt.float8e4
U32 = mybir.dt.uint32
U16 = mybir.dt.uint16

P = 128
EPS = 1e-5
B, T, E = 16, 64, 256
H, G, D = 8, 4, 8
NPAIR = B // 2
SCALE = float(D) ** -0.5
F = 4 * E
KT, FT = E // P, F // P
QKV = E + 2 * H * D
FP8_MAX = 448.0
TINY = 2.0 ** -5

C_COS, C_SIN, C_HEAD, C_ID, C_NUM, C_DEN, C_STEP, C_MASK, C_NUM2, C_DEN2 = 0, 8, 16, 24, 152, 408, 664, 728, 792, 856
C_END = 920
PARTS_Q = (0, 1, 2, 0, 1, 0)
PARTS_K = (0, 0, 0, 1, 1, 2)
SPLIT = len(PARTS_Q) * D
ROWS = SPLIT + 2


def build(nc, x, ctxt, ctxt_t, wqkv, bqkv, wo, bo, gamma, wfc, wproj, cf, cb, out):
    with ExitStack() as stack:
        def sb(name, shape, dt=F32):
            return stack.enter_context(nc.sbuf_tensor(name, shape, dt))

        def sem(name):
            return stack.enter_context(nc.semaphore(name))

        bank = [stack.enter_context(nc.psum_tensor(f"bank{i}", [P, 512], F32)) for i in range(2)]
        ps_a = stack.enter_context(nc.psum_tensor("ps_a", [P, 2, 512], F32))
        ps_t = stack.enter_context(nc.psum_tensor("ps_t", [P, 4, 512], F32))

        x_in = sb("x_in", [P, NPAIR, E])
        xb = sb("xb", [P, NPAIR, E])
        x1 = sb("x1", [P, NPAIR, E])
        x2 = sb("x2", [P, NPAIR, E])
        ctx_t = sb("ctx_t", [P, 2, B, T])
        const = sb("const", [P, C_END])
        constb = sb("constb", [P, P + 16 * T], BF16)
        w_qkv = sb("w_qkv", [P, KT, QKV])
        b_qkv = sb("b_qkv", [1, QKV])
        ones = sb("ones", [1, P])
        w_o = sb("w_o", [P, G, E])
        bo_bc = sb("bo_bc", [P, E])
        gam = sb("gam", [P, 1])
        neg_half = sb("neg_half", [P, 1])

        wf = sb("wf", [P, KT, F])
        wp = sb("wp", [P, FT, E])

        stats = sb("stats", [P, 2, 6])
        mv = sb("mv", [P, 2, 2])
        var = sb("var", [P, 2])
        rstd = sb("rstd", [P, 2])
        xn = sb("xn", [P, 2, E])
        xn_t = sb("xn_t", [P, 2, KT, P])
        rope_c = sb("rope_c", [P, QKV - H * D])
        rope_s = sb("rope_s", [P, QKV - H * D])
        qk = sb("qk", [P, 2, QKV - H * D])
        q_t = sb("q_t", [P, 2, 2, G, T])
        k_t = sb("k_t", [H * D, 2, P])
        hid_all = sb("hid_all", [P, FT * B * T])
        hid = hid_all[:].rearrange("p (f t) -> p f t", f=FT)
        quarter = [hid_all[:, 2048 * k:2048 * k + 2048] for k in range(4)]
        k_z = quarter[0].rearrange("p (u h b t) -> p u h b t", u=2, h=H, b=2)
        v_z = sb("v_z", [P, 2, H, 32])
        nmax = sb("nmax", [P, 2, 2, H, 2])
        nmax_p = sb("nmax_p", [P, 2, 2, 2, 16], BF16)
        nmax_t = sb("nmax_t", [P, 2, 2, P], BF16)
        probs = quarter[1].rearrange("p (s c q) -> p s c q", s=2, c=4)
        u_sb = sb("u_sb", [P, 2, 2, E])
        rden = sb("rden", [P, E])
        y_t = sb("y_t", [P, 2, E])
        stats2 = sb("stats2", [P, 6])
        mv2 = sb("mv2", [P, 2])
        var2 = sb("var2", [P, 1])
        rstd2 = sb("rstd2", [P, 1])
        x1n = sb("x1n", [P, 2, E])
        rest = sb("rest", [P, 2, E])
        q_parts = sb("q_parts", [P, 2, 3, E], BF16)
        ctx_in = sb("ctx_in", [P, NPAIR, E])
        ctx_rest = sb("ctx_rest", [P, E])
        k_parts = sb("k_parts", [P, 2, 3, E], BF16)
        d_q = nc.dram_tensor("d_q", [B * 4, 2, len(PARTS_Q), D, E], BF16, kind="Internal").ap()
        d_k = nc.dram_tensor("d_k", [B * 4, 2, len(PARTS_K), D, E], BF16, kind="Internal").ap()
        q_st, k_st = (quarter[k].bitcast(BF16).rearrange("p (r a e) -> p r a e", r=4, a=4) for k in (2, 3))
        v2_z = sb("v2_z", [P, 2, 2, H, 32])
        nmax2 = sb("nmax2", [P, 2, 2, 2, 4])
        nmax2_p = sb("nmax2_p", [P, 2, 2, 2, 2, 4], BF16)
        nmax2_t = sb("nmax2_t", [16, 2, 2, P], BF16)
        probs2_all = sb("probs2", [P, 4 * 2 * 2 * E])
        probs2 = probs2_all[:].rearrange("p (r h l q) -> p r h l q", r=4, h=2, l=2)
        u2_sb = sb("u2_sb", [P, 2, E])
        rden2 = sb("rden2", [P, E])
        y2 = sb("y2", [P, E])
        stats3 = sb("stats3", [P, NPAIR, 6])
        mv3 = sb("mv3", [P, NPAIR, 2])
        var3 = sb("var3", [P, NPAIR])
        rstd3 = sb("rstd3", [P, NPAIR])
        top = sb("top", [P, 4])
        top_all = sb("top_all", [P, 4])
        unit = sb("unit", [P, 4])
        inv = sb("inv", [P, 4])
        half_inv = sb("half_inv", [P, 1])
        step1 = sb("step1", [P, 1])
        step2 = sb("step2", [P, 1])
        quant = x_in[:].rearrange("p n d -> p (n d)")
        magic = ctx_in[:].rearrange("p n d -> p (n d)")
        wf8 = sb("wf8", [P, KT, F], BF16)
        wp8 = sb("wp8", [P, 2, FT, E], BF16)
        x8 = sb("x8", [P, NPAIR, E], BF16)
        x8_t = sb("x8_t", [P, KT, B * T], BF16)
        minus_tiny = sb("minus_tiny", [P, P], BF16)
        tops = sb("tops", [P, 2 * FT])
        h_lo, h_hi = (probs2_all[:, 2048 * k:2048 * k + 2048].bitcast(FP8).rearrange("p (f t) -> p f t", f=FT) for k in range(2))
        res = x1

        sems = {}

        def s(name):
            if name not in sems:
                sems[name] = sem(name)
            return sems[name]

        names = """ld_x ld_ctx ld_small ld_w ld_wo ld_ffn setup_pool setup_dve var_ready rstd_ready xn_ready
        xt_ps xt_ready proj_ready qk_ready qkt_ps qt_ready kt_ready kz_ready v_ready
        s_ready max_done nmax_ready mt_ps mt_ready t_ready exp_done u_ready us_ready nd_ready y_ready w_ready
        x1_ready var2_ready rstd2_ready x1n_ready parts_ready chain_a chain_b chain_c chain_p passed kparts_ready max2_done nmax2_ready mt2_ps mt2_ready
        s2_ready t2_ready exp2_done pv2_done v2_ready us2_ready nd2_ready nd2_read x2_ready var3_ready rstd3_ready top_ready top_all_ready x8_ready x8t_ps x8t_ready
        wp8_ready wf8_ready fc1_ready relu_ready hid_ready hq_ready bias_ps fc2_ready res_ready stored chain_f chain_m chain_k
        """.split()
        for n in names:
            s(n)
        q_written = [sem(f"q_written{u}") for u in range(2)]
        k_written = [sem(f"k_written{u}") for u in range(2)]
        qk_loaded = [sem(f"qk_loaded{r}") for r in range(4)]
        m_loaded = [sem(f"m_loaded{r}") for r in range(4)]
        block = stack.enter_context(nc.Block())

        def wait(eng, name, value, alone=False):
            if not isinstance(value, int) or value > 0:
                eng.wait_ge(s(name) if isinstance(name, str) else name, value)
                if alone and not isinstance(value, int):
                    eng.sem_inc(s("passed"), 1)

        def uses(n, par):
            return n + (2 - par)

        def steps(eng, body):
            for n in range(2):
                body(n, n, True)
            with eng.Fori(2, NPAIR - 3, 2) as i:
                for v in range(2):
                    body(i + v, v, True)
            for n in range(NPAIR - 2, NPAIR):
                body(n, n % 2, n + 1 < NPAIR)

        def steps2(eng, body):
            body(0, 0)
            with eng.Fori(1, B - 6, 4) as i:
                for v in range(4):
                    body(i + v, (1 + v) % 4)
            for n in range(B - 3, B):
                body(n, n % 4)

        def loads_of(n, r, each):
            return each // 4 * (n - r) + each

        def chained(eng, name, n, per_pair):
            done = [0]

            def link(ins, alone=False):
                done[0] += 1
                assert done[0] <= per_pair
                ins.then_inc(s(name), 1)
                wait(eng, name, n * per_pair + done[0], alone)
            return link

        tok = lambda ap: ap.rearrange("(n p) d -> p n d", p=P)

        def at(ap, n):
            return ap[:, n, :] if isinstance(n, int) else ap[:, bass.ds(n, 1), :]

        @block.sync
        def _(sp):
            sp.dma_start(x_in[:], tok(x)).then_inc(s("ld_x"), 16)
            sp.dma_start(const[:], cf).then_inc(s("ld_small"), 16)
            sp.dma_start(constb[:].bitcast(U16), cb).then_inc(s("ld_small"), 16)
            sp.dma_start(b_qkv[:], bqkv).then_inc(s("ld_small"), 16)
            sp.dma_start(w_qkv[:], wqkv.rearrange("(k p) n -> p k n", p=P)).then_inc(s("ld_w"), 16)
            sp.dma_start(bo_bc[:], bo.partition_broadcast(P)).then_inc(s("ld_wo"), 16)
            sp.dma_start(gam[:], gamma.partition_broadcast(P)).then_inc(s("ld_wo"), 16)
            for half in range(2):
                sp.dma_start(w_o[64 * half:64 * half + 64], wo).then_inc(s("ld_wo"), 16)
            sp.dma_start(wf[:], wfc.rearrange("(k p) n -> p k n", p=P)).then_inc(s("ld_ffn"), 16)
            sp.dma_start(wp[:], wproj.rearrange("(k p) n -> p k n", p=P)).then_inc(s("ld_ffn"), 16)
            sp.dma_start(ctx_in[:], tok(ctxt)).then_inc(s("ld_ctx"), 16)
            sp.dma_start(ctx_t[:], ctxt_t.rearrange("(l p) (b t) -> p l b t", p=P, t=T)).then_inc(s("ld_ctx"), 16)

            def spread(d_st, parts, src, n, written):
                rows = d_st.rearrange("(n a) h c d e -> n c (a h) d e", a=8)
                for c, part in enumerate(parts):
                    dst = rows[n, c] if isinstance(n, int) else rows[bass.ds(n, 1), c].rearrange("n a d e -> (n a) d e")
                    sp.dma_start(dst, src[:, part, :]).then_inc(written, 16)

            def body(n, u, more):
                wait(sp, "kparts_ready", n + 1)
                spread(d_k, PARTS_K, k_parts[:, u], n, k_written[u])
                wait(sp, "parts_ready", n + 1)
                spread(d_q, PARTS_Q, q_parts[:, u], n, q_written[u])
            steps(sp, body)
            for u in range(2):
                sp.wait_ge(q_written[u], 16 * 6 * 4)
                sp.wait_ge(k_written[u], 16 * 6 * 4)

            def load(n, r):
                for st, d_st in ((q_st, d_q), (k_st, d_k)):
                    for hp in range(2):
                        src = d_st[4 * n:4 * n + 4, hp] if isinstance(n, int) else d_st[bass.ds(4 * n, 4), hp]
                        sp.dma_start(st[64 * hp:64 * hp + SPLIT, r], src.rearrange("a c d e -> (c d) a e")
                                     ).then_inc(qk_loaded[r], 16)

            sp.wait_ge(s("setup_pool"), 19)
            for n in range(3):
                load(n, n)

            def body2(n, r):
                if isinstance(n, int) and n + 3 >= B:
                    return
                wait(sp, "t2_ready", 4 * n)
                load(n + 3, (r + 3) % 4)
            steps2(sp, body2)
            for n in range(NPAIR):
                sp.wait_ge(s("res_ready"), n + 1)
                sp.dma_start(tok(out)[:, n, :], res[:, n, :]).then_inc(s("stored"), 16)
            sp.wait_ge(s("stored"), 16 * NPAIR)

        @block.gpsimd
        def _(pool):
            nc.gpsimd.memset(ones[:], 1.0).then_inc(s("setup_pool"), 1)
            nc.gpsimd.memset(neg_half[:], -0.5).then_inc(s("setup_pool"), 1)
            nc.gpsimd.memset(nmax_t[:], 0.0).then_inc(s("setup_pool"), 1)
            for u in range(2):
                nc.gpsimd.memset(v_z[:, u], 0.0).then_inc(s("setup_pool"), 1)
            pool.wait_ge(s("setup_pool"), 5)
            for u in range(2):
                nc.gpsimd.memset(v_z[0:64, u, :, 8:16], 1.0).then_inc(s("setup_pool"), 1)
            for u in range(2):
                pool.wait_ge(s("setup_pool"), 7 + u)
                nc.gpsimd.memset(v_z[64:128, u, :, 24:32], 1.0).then_inc(s("setup_pool"), 1)
            pool.wait_ge(s("ld_small"), 48)
            pool.wait_ge(s("setup_pool"), 9)
            for u in range(2):
                nc.gpsimd.tensor_copy(q_t[64:128, u].rearrange("p b g t -> p (b g) t"),
                                      const[64:128, C_STEP:C_STEP + T].unsqueeze(1).to_broadcast([64, 2 * G, T])
                                      ).then_inc(s("setup_pool"), 1)
                nc.gpsimd.tensor_copy(k_z[64:128, u].rearrange("p h b t -> p (h b) t"),
                                      const[64:128, C_MASK:C_MASK + T].unsqueeze(1).to_broadcast([64, 2 * H, T])
                                      ).then_inc(s("setup_pool"), 1)
            pool.wait_ge(s("setup_pool"), 13)
            nc.gpsimd.memset(v2_z[:], 0.0).then_inc(s("setup_pool"), 1)
            pool.wait_ge(s("setup_pool"), 14)
            for hh in range(2):
                for u in range(2):
                    nc.gpsimd.memset(v2_z[:, u, :, 4 * hh:4 * hh + 4, 16 * hh + 8:16 * hh + 16], 1.0).then_inc(s("setup_pool"), 1)
            nc.gpsimd.memset(k_st[:], 1.0).then_inc(s("setup_pool"), 1)
            pool.wait_ge(s("setup_pool"), 19)

            def rstd_a(n, u):
                wait(pool, "var_ready", n + 1)
                nc.gpsimd.tensor_tensor(rstd[:, u:u + 1], var[:, u:u + 1], neg_half[:], ALU.pow).then_inc(s("rstd_ready"), 1)

            def heads_a(n, u):
                wait(pool, "kt_ready", n + 1)
                wait(pool, "t_ready", 2 * (n - 1))
                nc.gpsimd.tensor_tensor(
                    k_z[0:64, u].rearrange("p h b t -> p h (b t)"),
                    k_t[:, u, :].unsqueeze(1).to_broadcast([64, H, P]),
                    const[0:64, C_HEAD:C_HEAD + H].unsqueeze(2).to_broadcast([64, H, P]), ALU.mult).then_inc(s("kz_ready"), 1)

            def body(n, u, more):
                context(n, u)
                if more:
                    rstd_a(n + 1, 1 - u)
                    heads_a(n + 1, 1 - u)
                link = chained(pool, "chain_p", n, 3)
                wait(pool, "var2_ready", n + 1)
                nc.gpsimd.tensor_tensor(rstd2[:], var2[:], neg_half[:], ALU.pow).then_inc(s("rstd2_ready"), 1)
                wait(pool, "x1n_ready", n + 1)
                wait(pool, q_written[u], 48 * (n - u), alone=True)
                link(nc.gpsimd.tensor_copy(q_parts[:, u, 0, :], x1n[:, u, :]))
                link(nc.gpsimd.tensor_tensor(rest[:, u, :], x1n[:, u, :], q_parts[:, u, 0, :], ALU.subtract), alone=True)
                link(nc.gpsimd.tensor_copy(q_parts[:, u, 1, :], rest[:, u, :]))
                nc.gpsimd.tensor_tensor(q_parts[:, u, 2, :], rest[:, u, :], q_parts[:, u, 1, :], ALU.subtract).then_inc(s("parts_ready"), 1)

            def context(n, u):
                link = chained(pool, "chain_k", n, 3)
                wait(pool, k_written[u], 48 * (n - u), alone=True)
                c_n = at(ctx_in, n)
                k0, k1, k2 = (k_parts[:, u, c, :] if isinstance(n, int) else k_parts[:, u, c:c + 1, :] for c in range(3))
                r_n = ctx_rest[:] if isinstance(n, int) else ctx_rest[:].unsqueeze(1)
                link(nc.gpsimd.tensor_copy(k0, c_n), alone=True)
                link(nc.gpsimd.tensor_tensor(r_n, c_n, k0, ALU.subtract), alone=True)
                link(nc.gpsimd.tensor_copy(k1, r_n), alone=True)
                nc.gpsimd.tensor_tensor(k2, r_n, k1, ALU.subtract).then_inc(s("kparts_ready"), 1)

            rstd_a(0, 0)
            pool.wait_ge(s("ld_wo"), 64)
            nc.gpsimd.tensor_tensor(xb[:], x_in[:], bo_bc[:].unsqueeze(1).to_broadcast([P, NPAIR, E]), ALU.add).then_inc(s("setup_pool"), 1)
            heads_a(0, 0)
            pool.wait_ge(s("ld_ctx"), 32)
            steps(pool, body)

            def values(n, u):
                wait(pool, "pv2_done", 2 * (n - 1))
                for hh in range(2):
                    src = ctx_t[:, :, n, 32 * hh:32 * hh + 32] if isinstance(n, int) else ctx_t[:, :, bass.ds(n, 1), 32 * hh:32 * hh + 32].rearrange("p l n d -> p l (n d)")
                    ins = nc.gpsimd.tensor_copy(v2_z[:, u, :, 4 * hh:4 * hh + 4, 16 * hh:16 * hh + D], src.rearrange("p l (c d) -> p l c d", d=D))
                ins.then_inc(s("v2_ready"), 1)

            def maxima(n, r):
                wait(pool, "mt2_ready", n + 1, alone=True)
                for hp in range(2):
                    for part in range(2):
                        src = nmax2_t[8 * hp + 4 * part:8 * hp + 4 * part + 4, r % 2].rearrange("p g q -> p (g q)")
                        row = 64 * hp + SPLIT + part
                        pool.dma_start(q_st[row:row + 1, r], src).then_inc(m_loaded[r], 16)

            values(0, 0)
            values(1, 1)
            maxima(0, 0)

            def body2(n, r):
                if not isinstance(n, int) or n + 1 < B:
                    maxima(n + 1, (r + 1) % 4)
                if not isinstance(n, int) or n + 2 < B:
                    values(n + 2, r % 2)
            steps2(pool, body2)

            nc.gpsimd.memset(minus_tiny[:], -TINY).then_inc(s("setup_pool"), 1)
            for k in range(4):
                if k == 2:
                    pool.wait_ge(s("var3_ready"), 1)
                    nc.gpsimd.tensor_tensor(rstd3[:], var3[:], neg_half[:].to_broadcast([P, NPAIR]), ALU.pow).then_inc(s("rstd3_ready"), 1)
                pool.wait_ge(s("top_ready"), k + 1)
                nc.gpsimd.partition_all_reduce(top_all[:, k:k + 1], top[:, k:k + 1], P, bass.bass_isa.ReduceOp.max
                                               ).then_inc(s("top_all_ready"), 1)

        @block.tensor
        def _(pe):
            ident = const[:, C_ID:C_ID + P]
            pe.wait_ge(s("ld_small"), 48)
            pe.wait_ge(s("ld_w"), 16)
            pe.wait_ge(s("setup_pool"), 13)
            pe.wait_ge(s("ld_wo"), 64)

            def stage_a(n, u):
                wait(pe, "xn_ready", n + 1)
                wait(pe, "kt_ready", n)
                for k in range(KT):
                    mm = nc.tensor.transpose(bank[0][:, P * k:P * k + P], xn[:, u, P * k:P * k + P], ident)
                mm.then_inc(s("xt_ps"), 1)
                wait(pe, "xt_ready", n + 1)
                wait(pe, "v_ready", n)
                nc.tensor.matmul(bank[1][:, 0:QKV], ones[:], b_qkv[:], start=True, stop=False)
                for k in range(KT):
                    mm = nc.tensor.matmul(bank[1][:, 0:QKV], xn_t[:, u, k, :], w_qkv[:, k, :], start=False, stop=(k == KT - 1))
                mm.then_inc(s("proj_ready"), 1)
                wait(pe, "qk_ready", n + 1)
                wait(pe, "qt_ready", n, alone=True)
                for g in range(G):
                    nc.tensor.transpose(ps_a[0:64, 0, P * g:P * g + P], qk[:, u, 64 * g:64 * g + 64], ident)
                nc.tensor.transpose(bank[0][0:64, 2 * P:3 * P], qk[:, u, E:E + 64], ident).then_inc(s("qkt_ps"), 1)

            def stage_b(n, u):
                wait(pe, "qt_ready", n + 1)
                wait(pe, "kz_ready", n + 1)
                for b in range(2):
                    for gp in range(2):
                        k = 2 * b + gp
                        if k == 0:
                            wait(pe, "x1_ready", n)
                        if k == 1:
                            wait(pe, "x1_ready", n)
                        if k >= 2:
                            wait(pe, "max_done", 4 * n + k - 1)
                        nc.tensor.matmul(ps_t[:, 2 + k % 2, :], q_t[:, u, b, 2 * gp:2 * gp + 2, :].rearrange("p g t -> p (g t)"),
                                         k_z[:, u, :, b, :], start=True, stop=True).then_inc(s("s_ready"), 1)
                wait(pe, "nmax_ready", n + 1)
                pst = ps_t[0:32, 2, 0:P].bitcast(BF16)
                for gp in range(2):
                    mm = nc.tensor.transpose(pst[:, P * gp:P * gp + P], nmax_p[:, u, gp].rearrange("p a b -> p (a b)"), constb[:, 0:P])
                mm.then_inc(s("mt_ps"), 1)
                wait(pe, "mt_ready", n + 1)
                wait(pe, "v_ready", n + 1)
                for hh in range(2):
                    wait(pe, "exp_done", 2 * n + hh)
                    for c in range(4):
                        for b in range(2):
                            h = 4 * hh + c
                            o = ps_t[64 * b:64 * b + 64, c // 2, E * (c % 2):E * (c % 2) + E]
                            nc.tensor.matmul(o, k_z[:, u, h, b, :], q_t[:, u, b].rearrange("p g t -> p (g t)"),
                                             start=True, stop=False)
                            j = 2 * h + b
                            mm = nc.tensor.matmul(o, constb[:, P + T * j:P + T * j + T],
                                                  nmax_t[:, u].rearrange("p g q -> p (g q)"), start=False, stop=True)
                    mm.then_inc(s("t_ready"), 1)
                    wait(pe, "exp_done", 2 * n + hh + 1)
                    for c in range(4):
                        mm = nc.tensor.matmul(ps_a[32 * c:32 * c + 32, 1, E * hh:E * hh + E], v_z[:, u, 4 * hh + c, :],
                                              probs[:, hh, c, :], start=True, stop=True)
                mm.then_inc(s("u_ready"), 1)
                wait(pe, "us_ready", n + 1)
                for k, col in enumerate((C_NUM, C_DEN)):
                    for hh in range(2):
                        mm = nc.tensor.matmul(ps_a[:, 1, E * k:E * k + E], const[:, col + P * hh:col + P * hh + P],
                                              u_sb[:, u, hh, :], start=(hh == 0), stop=(hh == 1))
                mm.then_inc(s("nd_ready"), 1)
                wait(pe, "y_ready", n + 1, alone=True)
                for g in range(G):
                    for b in range(2):
                        r = slice(64 * b, 64 * b + 64)
                        mm = nc.tensor.matmul(ps_t[r, 3, 0:E], y_t[r, u, T * g:T * g + T], w_o[r, g, :],
                                              start=(g == 0), stop=(g == G - 1))
                mm.then_inc(s("w_ready"), 1)

            stage_a(0, 0)

            def body(n, u, more):
                if more:
                    stage_a(n + 1, 1 - u)
                stage_b(n, u)
            steps(pe, body)

            def scores(n, r, ht):
                if ht == 0:
                    wait(pe, qk_loaded[r], loads_of(n, r, 64))
                for hp in range(2):
                    wait(pe, "max2_done", 8 * n + 2 * ht + hp - 1)
                    rows = slice(64 * hp, 64 * hp + SPLIT)
                    for half in range(2):
                        mm = nc.tensor.matmul(bank[hp][:, E * half:E * half + E], q_st[rows, r, ht, P * half:P * half + P],
                                              k_st[rows, r, ht, :], start=True, stop=True)
                    mm.then_inc(s("s2_ready"), 1)

            def turn_maxima(n, r):
                wait(pe, "nmax2_ready", n + 1)
                wait(pe, "nd2_read", n - 1 - r % 2)
                dst = ps_a[0:16, 1, 0:P].bitcast(BF16)
                for half in range(2):
                    mm = nc.tensor.transpose(dst[:, P * half:P * half + P],
                                             nmax2_p[:, r % 2, half].rearrange("p h c t -> p (h c t)"), constb[:, 0:P])
                mm.then_inc(s("mt2_ps"), 1)

            def scores_t(n, r, ht):
                if ht == 0:
                    wait(pe, m_loaded[r], loads_of(n, r, 64))
                wait(pe, "exp2_done", 4 * n + ht - 1)
                for hp in range(2):
                    rows = slice(64 * hp, 64 * hp + ROWS)
                    for half in range(2):
                        mm = nc.tensor.matmul(ps_t[:, 2 * (ht % 2) + hp, E * half:E * half + E],
                                              k_st[rows, r, ht, P * half:P * half + P], q_st[rows, r, ht, :], start=True, stop=True)
                mm.then_inc(s("t2_ready"), 1)

            def weigh(n, r, hh):
                b = r % 2
                wait(pe, "exp2_done", 4 * n + 2 * hh + 2)
                if hh == 0:
                    wait(pe, "v2_ready", n + 1)
                    if b == 0:
                        wait(pe, "us2_ready", n)
                for half in range(2):
                    for c in range(4):
                        mm = nc.tensor.matmul(ps_a[32 * c:32 * c + 32, 0, E * b:E * b + E], v2_z[:, b, half, 4 * hh + c, :],
                                              probs2[:, 2 * hh + c // 2, c % 2, half, :],
                                              start=(b == 0 and hh == 0 and half == 0), stop=(hh == 1 and half == 1),
                                              skip_group_check=True)
                mm.then_inc(s("pv2_done"), 1)

            def gather_heads(n):
                wait(pe, "us2_ready", n)
                wait(pe, "mt2_ready", n + 2 if not isinstance(n, int) else min(n + 2, B))
                wait(pe, "nd2_read", n - 1)
                for k, col in enumerate((C_NUM2, C_DEN2)):
                    for b in range(2):
                        mm = nc.tensor.matmul(ps_a[64 * b:64 * b + 64, 1, E * k:E * k + E], const[:, col:col + 64],
                                              u2_sb[:, b, :], start=True, stop=True)
                    mm.then_inc(s("nd2_ready"), 1)

            pe.wait_ge(s("x1_ready"), NPAIR)
            pe.sem_inc(s("nd2_ready"), 1)
            for n in range(2):
                for ht in range(4):
                    scores(n, n, ht)
            turn_maxima(0, 0)

            def body2(n, r):
                known = isinstance(n, int)
                ahead = not known or n + 2 < B
                if ahead:
                    scores(n + 2, (r + 2) % 4, 0)
                scores_t(n, r, 0)
                if not known or n + 1 < B:
                    turn_maxima(n + 1, (r + 1) % 4)
                if not known or n > 0:
                    weigh(n - 1, (r - 1) % 4, 1)
                if ahead:
                    scores(n + 2, (r + 2) % 4, 1)
                scores_t(n, r, 1)
                if r % 2 == 0 and (not known or n > 0):
                    gather_heads(n)
                if ahead:
                    scores(n + 2, (r + 2) % 4, 2)
                scores_t(n, r, 2)
                weigh(n, r, 0)
                if ahead:
                    scores(n + 2, (r + 2) % 4, 3)
                scores_t(n, r, 3)
            steps2(pe, body2)
            weigh(B - 1, 3, 1)
            gather_heads(B)

            pe.wait_ge(s("x2_ready"), NPAIR)
            pe.wait_ge(s("setup_pool"), 21)
            for n in range(NPAIR):
                pe.wait_ge(s("x8_ready"), 1)
                for k in range(KT):
                    mm = nc.tensor.transpose(bank[k][:].bitcast(BF16)[:, P * n:P * n + P], x8[:, n, P * k:P * k + P], constb[:, 0:P])
            mm.then_inc(s("x8t_ps"), 1)
            pe.wait_ge(s("wp8_ready"), 1)
            for f in range(FT):
                mm = nc.tensor.matmul(ps_a[:, 0, 0:E], minus_tiny[:], wp8[:, 0, f, :], start=(f == 0), stop=(f == FT - 1))
            mm.then_inc(s("bias_ps"), 1)
            pe.wait_ge(s("wf8_ready"), 1)
            pe.wait_ge(s("x8t_ready"), 2)
            for i in range(2 * FT):
                f, half = i // 2, i % 2
                if i >= 4:
                    pe.wait_ge(s("relu_ready"), i - 3)
                for k in range(KT):
                    mm = nc.tensor.matmul(ps_t[:, i % 4, :], wf8[:, k, P * f:P * f + P], x8_t[:, k, 512 * half:512 * half + 512],
                                          start=(k == 0), stop=(k == KT - 1))
                mm.then_inc(s("fc1_ready"), 1)
            pe.wait_ge(s("relu_ready"), 2 * FT)
            for n in range(NPAIR):
                pe.wait_ge(s("hq_ready"), 2 * (n // 4 + 1))
                if n >= 4:
                    pe.wait_ge(s("res_ready"), n - 3)
                for part, h8 in enumerate((h_lo, h_hi)):
                    for f in range(FT):
                        mm = nc.tensor.matmul(ps_t[:, n % 4, 0:E], h8[:, f, P * n:P * n + P], wp8[:, part, f, :],
                                              start=(part == 0 and f == 0), stop=(part == 1 and f == FT - 1))
                mm.then_inc(s("fc2_ready"), 1)

        @block.scalar
        def _(act):
            def stage_a(n, u):
                wait(act, "xt_ps", n + 1)
                nc.scalar.copy(xn_t[:, u].rearrange("p k t -> p (k t)"), bank[0][:, 0:2 * P]).then_inc(s("xt_ready"), 1)
                wait(act, "qk_ready", n + 1)
                wait(act, "u_ready", n - 1)
                for b in range(2):
                    r = slice(64 * b, 64 * b + 64)
                    ins = nc.scalar.copy(v_z[r, u, :, 16 * b:16 * b + D],
                                         bank[1][r, E + 64:QKV].rearrange("p (h d) -> p h d", d=D))
                ins.then_inc(s("v_ready"), 1)
                wait(act, "qkt_ps", n + 1)
                nc.scalar.copy(k_t[:, u, :], bank[0][0:64, 2 * P:3 * P]).then_inc(s("kt_ready"), 1)
                wait(act, "t_ready", 2 * (n - 1))
                for b in range(2):
                    ins = nc.scalar.copy(q_t[0:64, u, b], ps_a[0:64, 0, :].rearrange("p (g b t) -> p b g t", b=2, t=T)[:, b])
                ins.then_inc(s("qt_ready"), 1)

            def stage_b(n, u):
                wait(act, "mt_ps", n + 1)
                nc.scalar.copy(nmax_t[0:32, u].rearrange("p g q -> p (g q)"), ps_t[0:32, 2, 0:P].bitcast(BF16)).then_inc(s("mt_ready"), 1)
                for hh in range(2):
                    wait(act, "t_ready", 2 * n + hh + 1)
                    nc.scalar.activation(probs[:, hh].rearrange("p c q -> p (c q)"),
                                         ps_t[:, 0:2, :].rearrange("p a b -> p (a b)"), ACT.Exp, scale=SCALE).then_inc(s("exp_done"), 1)
                wait(act, "u_ready", n + 1)
                nc.scalar.copy(u_sb[:, u].rearrange("p b q -> p (b q)"), ps_a[:, 1, :]).then_inc(s("us_ready"), 1)

            stage_a(0, 0)

            def body(n, u, more):
                if more:
                    stage_a(n + 1, 1 - u)
                stage_b(n, u)
            steps(act, body)

            def exp2(n, r, ht):
                wait(act, "t2_ready", 4 * n + ht + 1)
                wait(act, "pv2_done", 2 * (n - 1) + ht // 2 + 1)
                b = 2 * (ht % 2)
                nc.scalar.activation(probs2[:, ht].rearrange("p h l q -> p (h l q)"),
                                     ps_t[:, b:b + 2, :].rearrange("p a b -> p (a b)"), ACT.Exp, scale=SCALE).then_inc(s("exp2_done"), 1)

            def keep_maxima(n, r):
                wait(act, "mt2_ps", n + 1)
                nc.scalar.copy(nmax2_t[:, r % 2].rearrange("p g q -> p (g q)"), ps_a[0:16, 1, 0:P].bitcast(BF16)).then_inc(s("mt2_ready"), 1)

            def keep_sums(n):
                wait(act, "pv2_done", 2 * n)
                wait(act, "nd2_ready", n - 1)
                for b in range(2):
                    nc.scalar.copy(u2_sb[:, b, :], ps_a[:, 0, E * b:E * b + E]).then_inc(s("us2_ready"), 1)

            keep_maxima(0, 0)

            def body2(n, r):
                known = isinstance(n, int)
                exp2(n, r, 0)
                if not known or n + 1 < B:
                    keep_maxima(n + 1, (r + 1) % 4)
                exp2(n, r, 1)
                if r % 2 == 0 and (not known or n > 0):
                    keep_sums(n)
                exp2(n, r, 2)
                exp2(n, r, 3)
            steps2(act, body2)
            keep_sums(B)

            act.wait_ge(s("x8t_ps"), 1)
            for k in range(KT):
                nc.scalar.copy(x8_t[:, k, :], bank[k][:].bitcast(BF16)).then_inc(s("x8t_ready"), 1)
            for i in range(2 * FT):
                f, half = i // 2, i % 2
                part = hid[:, f, 512 * half:512 * half + 512]
                act.wait_ge(s("relu_ready"), i + 1)
                nc.scalar.activation(part, part, ACT.Square, scale=step1[:, 0:1]).then_inc(s("hid_ready"), 1)

        @block.vector
        def _(dve):
            NQ = QKV - H * D

            def stage_a(n, u):
                link = chained(dve, "chain_a", n, 5)
                link(nc.vector.bn_stats(stats[:, u, :], at(x_in, n)), alone=True)
                link(nc.vector.bn_aggr(mv[:, u, :], stats[:, u, :]))
                nc.vector.tensor_scalar(var[:, u:u + 1], mv[:, u, 1:2], EPS, None, ALU.add).then_inc(s("var_ready"), 1)
                wait(dve, "rstd_ready", n + 1)
                nc.vector.tensor_scalar(xn[:, u, :], at(x_in, n), mv[:, u, 0:1], rstd[:, u:u + 1], ALU.subtract, ALU.mult).then_inc(s("xn_ready"), 1)
                wait(dve, "proj_ready", n + 1)
                heads = bank[1][:, 0:NQ].rearrange("p (a d) -> p a d", d=D)
                sh = rope_s[:].rearrange("p (a d) -> p a d", d=D)
                link(nc.vector.tensor_tensor(rope_c[:].rearrange("p (a d) -> p a d", d=D), heads,
                                             const[:, C_COS:C_COS + D].unsqueeze(1).to_broadcast([P, NQ // D, D]), ALU.mult))
                link(nc.vector.tensor_tensor(sh[:, :, 0:4], heads[:, :, 4:8],
                                             const[:, C_SIN:C_SIN + 4].unsqueeze(1).to_broadcast([P, NQ // D, 4]), ALU.mult))
                link(nc.vector.tensor_tensor(sh[:, :, 4:8], heads[:, :, 0:4],
                                             const[:, C_SIN + 4:C_SIN + 8].unsqueeze(1).to_broadcast([P, NQ // D, 4]), ALU.mult))
                nc.vector.tensor_tensor(qk[:, u, :], rope_c[:], rope_s[:], ALU.add).then_inc(s("qk_ready"), 1)

            def stage_b(n, u):
                link = chained(dve, "chain_b", n, 4)
                for k in range(4):
                    b, gp = k // 2, k % 2
                    wait(dve, "s_ready", 4 * n + k + 1)
                    nc.vector.tensor_reduce(nmax[:, u, gp, :, b], ps_t[:, 2 + k % 2, :].rearrange("p (h t) -> p h t", t=T), AX.X, ALU.max,
                                            negate=True).then_inc(s("max_done"), 1)
                wait(dve, "max_done", 4 * n + 4)
                flat = nmax[:, u].rearrange("p g h b -> p g (h b)")
                link(nc.vector.tensor_copy(nmax_p[:, u, :, 0, :], flat))
                nc.vector.tensor_tensor(nmax_p[:, u, :, 1, :], flat, nmax_p[:, u, :, 0, :], ALU.subtract).then_inc(s("nmax_ready"), 1)
                wait(dve, "nd_ready", n + 1)
                link(nc.vector.reciprocal(rden[:], ps_a[:, 1, E:2 * E]))
                nc.vector.tensor_tensor(y_t[:, u, :], ps_a[:, 1, 0:E], rden[:], ALU.mult).then_inc(s("y_ready"), 1)
                wait(dve, "w_ready", n + 1)
                x1_n = at(x1, n)
                nc.vector.tensor_tensor(x1_n, ps_t[:, 3, 0:E] if isinstance(n, int) else ps_t[:, 3:4, 0:E], at(xb, n), ALU.add).then_inc(s("x1_ready"), 1)
                wait(dve, "x1_ready", n + 1, alone=True)
                link(nc.vector.bn_stats(stats2[:], x1_n), alone=True)
                link(nc.vector.bn_aggr(mv2[:], stats2[:]))
                nc.vector.tensor_scalar(var2[:], mv2[:, 1:2], EPS, None, ALU.add).then_inc(s("var2_ready"), 1)
                wait(dve, "rstd2_ready", n + 1)
                wait(dve, "parts_ready", n - 1)
                nc.vector.tensor_scalar(x1n[:, u, :] if isinstance(n, int) else x1n[:, u:u + 1, :], x1_n, mv2[:, 0:1], rstd2[:],
                                        ALU.subtract, ALU.mult).then_inc(s("x1n_ready"), 1)

            dve.wait_ge(s("ld_x"), 16)
            dve.wait_ge(s("ld_small"), 48)
            stage_a(0, 0)
            dve.wait_ge(s("setup_pool"), 20)

            def body(n, u, more):
                if more:
                    stage_a(n + 1, 1 - u)
                stage_b(n, u)
            steps(dve, body)

            dve.sem_inc(s("nd2_read"), 1)

            def maxima(n, r, ht):
                for hp in range(2):
                    wait(dve, "s2_ready", 8 * n + 2 * ht + hp + 1)
                    nc.vector.tensor_reduce(nmax2[:, r % 2, :, hp, ht], bank[hp][:].rearrange("p (a k) -> p a k", k=E), AX.X, ALU.max,
                                            negate=True).then_inc(s("max2_done"), 1)

            def split_maxima(n, r):
                link = chained(dve, "chain_m", n, 1)
                wait(dve, "max2_done", 8 * n + 8)
                wait(dve, "mt2_ps", n - 1)
                link(nc.vector.tensor_copy(nmax2_p[:, r % 2, :, :, 0, :], nmax2[:, r % 2]))
                nc.vector.tensor_tensor(nmax2_p[:, r % 2, :, :, 1, :], nmax2[:, r % 2], nmax2_p[:, r % 2, :, :, 0, :], ALU.subtract).then_inc(s("nmax2_ready"), 1)

            def finish(n):
                known = isinstance(n, int)
                cols = slice(P * (n - 2), P * n) if known else bass.ds(P * (n - 2), 2 * P)
                flat = [a[:].rearrange("p n d -> p (n d)")[:, cols] for a in (x1, x2)]
                wait(dve, "nd2_ready", n + 1)
                nc.vector.reciprocal(rden2[:], ps_a[:, 1, E:2 * E]).then_inc(s("nd2_read"), 1)
                wait(dve, "nd2_read", n)
                nc.vector.tensor_tensor(y2[:], ps_a[:, 1, 0:E], rden2[:], ALU.mult).then_inc(s("nd2_read"), 1)
                wait(dve, "nd2_read", n + 1)
                nc.vector.scalar_tensor_tensor(out=flat[1], in0=y2[:], scalar=gam[:, 0:1], in1=flat[0], op0=ALU.mult, op1=ALU.add
                                               ).then_inc(s("x2_ready"), 1)

            for n in range(2):
                for ht in range(4):
                    maxima(n, n, ht)
                split_maxima(n, n)

            def body2(n, r):
                known = isinstance(n, int)
                ahead = not known or n + 2 < B
                if ahead:
                    for ht in range(2):
                        maxima(n + 2, (r + 2) % 4, ht)
                if r % 2 == 0 and (not known or n > 0):
                    finish(n)
                if ahead:
                    for ht in range(2, 4):
                        maxima(n + 2, (r + 2) % 4, ht)
                    split_maxima(n + 2, (r + 2) % 4)
            steps2(dve, body2)
            finish(B)

            link = chained(dve, "chain_f", 0, 100)

            def scale_of(k):
                dve.wait_ge(s("top_all_ready"), k + 1)
                link(nc.vector.tensor_scalar(unit[:, k:k + 1], top_all[:, k:k + 1], 1.0 / FP8_MAX, 1e-6, ALU.mult, ALU.max))
                link(nc.vector.reciprocal(inv[:, k:k + 1], unit[:, k:k + 1]))

            def round_fp8(dst, src, k):
                link(nc.vector.tensor_scalar(quant, src, inv[:, k:k + 1], None, ALU.mult))
                link(nc.vector.tensor_scalar(magic.bitcast(U32), quant.bitcast(U32), 0x7F800000, None, ALU.bitwise_and))
                link(nc.vector.tensor_scalar(magic, magic, 2.0 ** -6, 1.5 * 2.0 ** 20, ALU.max, ALU.mult))
                link(nc.vector.tensor_tensor(quant, quant, magic, ALU.add))
                return nc.vector.tensor_tensor(dst, quant, magic, ALU.subtract)

            dve.wait_ge(s("ld_ffn"), 32)
            for k, w in enumerate((wf, wp)):
                nc.vector.tensor_reduce(top[:, k:k + 1], w[:].rearrange("p k n -> p (k n)"), AX.X, ALU.max, apply_absolute_value=True
                                        ).then_inc(s("top_ready"), 1)
            scale_of(0)
            round_fp8(wf8[:].rearrange("p k n -> p (k n)"), wf[:].rearrange("p k n -> p (k n)"), 0).then_inc(s("wf8_ready"), 1)
            dve.wait_ge(s("wf8_ready"), 1)
            scale_of(1)
            link(round_fp8(wp8[:, 0].rearrange("p k n -> p (k n)"), wp[:].rearrange("p k n -> p (k n)"), 1))
            nc.vector.tensor_scalar(wp8[:, 1], wp8[:, 0], 2.0, None, ALU.mult).then_inc(s("wp8_ready"), 1)
            dve.wait_ge(s("x2_ready"), NPAIR)
            for n in range(NPAIR):
                ins = nc.vector.bn_stats(stats3[:, n, :], x2[:, n, :])
            link(ins)
            for n in range(NPAIR):
                ins = nc.vector.bn_aggr(mv3[:, n, :], stats3[:, n, :])
            link(ins)
            nc.vector.tensor_scalar(var3[:], mv3[:, :, 1], EPS, None, ALU.add).then_inc(s("var3_ready"), 1)
            dve.wait_ge(s("rstd3_ready"), 1)
            for n in range(NPAIR):
                ins = nc.vector.tensor_scalar(xb[:, n, :], x2[:, n, :], mv3[:, n, 0:1], rstd3[:, n:n + 1], ALU.subtract, ALU.mult)
            link(ins)
            xn_all = xb[:].rearrange("p n d -> p (n d)")
            nc.vector.tensor_reduce(top[:, 2:3], xn_all, AX.X, ALU.max, apply_absolute_value=True).then_inc(s("top_ready"), 1)
            scale_of(2)
            link(nc.vector.tensor_tensor(step1[:], unit[:, 0:1], unit[:, 2:3], ALU.mult))
            round_fp8(x8[:].rearrange("p n d -> p (n d)"), xn_all, 2).then_inc(s("x8_ready"), 1)
            for i in range(2 * FT):
                f, half = i // 2, i % 2
                dve.wait_ge(s("fc1_ready"), i + 1)
                nc.vector.tensor_scalar(hid[:, f, 512 * half:512 * half + 512], ps_t[:, i % 4, :], 0.0, None, ALU.max, ALU.max,
                                        accum_out=tops[:, i:i + 1]).then_inc(s("relu_ready"), 1)
            dve.wait_ge(s("relu_ready"), 2 * FT)
            link(nc.vector.tensor_reduce(top[:, 3:4], tops[:], AX.X, ALU.max))
            link(nc.vector.tensor_tensor(top[:, 3:4], top[:, 3:4], step1[:], ALU.mult))
            nc.vector.tensor_tensor(top[:, 3:4], top[:, 3:4], top[:, 3:4], ALU.mult).then_inc(s("top_ready"), 1)
            scale_of(3)
            link(nc.vector.tensor_scalar(half_inv[:], inv[:, 3:4], 0.5, None, ALU.mult))
            link(nc.vector.tensor_tensor(step2[:], unit[:, 1:2], unit[:, 3:4], ALU.mult))
            dve.wait_ge(s("hid_ready"), 2 * FT)
            for half in range(2):
                c = slice(512 * half, 512 * half + 512)
                nc.vector.tensor_scalar(h_lo[:, :, c], hid[:, :, c], inv[:, 3:4], TINY, ALU.mult, ALU.min, saturate=False).then_inc(s("hq_ready"), 1)
                nc.vector.tensor_scalar(h_hi[:, :, c], hid[:, :, c], half_inv[:], TINY / 2, ALU.mult, ALU.max, saturate=False).then_inc(s("hq_ready"), 1)
            dve.wait_ge(s("bias_ps"), 1)
            link(nc.vector.scalar_tensor_tensor(out=xb[:], in0=ps_a[:, 0, 0:E].unsqueeze(1).to_broadcast([P, NPAIR, E]), scalar=step2[:, 0:1],
                                                in1=x2[:], op0=ALU.mult, op1=ALU.add))
            for n in range(NPAIR):
                dve.wait_ge(s("fc2_ready"), n + 1)
                nc.vector.scalar_tensor_tensor(out=res[:, n, :], in0=ps_t[:, n % 4, 0:E], scalar=step2[:, 0:1], in1=xb[:, n, :],
                                               op0=ALU.mult, op1=ALU.add).then_inc(s("res_ready"), 1)


def constants():
    import numpy as np
    f = np.float32
    c = np.zeros((P, C_END), f)
    j = np.arange(D // 2, dtype=f)
    theta = f(10000.0) ** (f(-2.0) * j / f(D))
    ang = (np.arange(T, dtype=f) + f(1.0))[:, None] * theta[None, :].astype(f)
    ang = np.concatenate([ang, ang], -1)
    c[:, C_COS:C_COS + D] = np.tile(np.cos(ang), (2, 1))
    sin = np.sin(ang)
    sin[:, :D // 2] *= -1
    c[:, C_SIN:C_SIN + D] = np.tile(sin, (2, 1))
    for h in range(H):
        c[D * h:D * h + D, C_HEAD + h] = 1.0
    c[:, C_ID:C_ID + P] = np.eye(P, dtype=f)
    for b in range(2):
        for h in range(H):
            for d in range(D):
                row, col = 32 * (h % 4) + 16 * b + d, P * (h // 4) + 64 * b + D * h + d
                c[row, C_NUM + col] = 1.0
                c[row + D, C_DEN + col] = 1.0
    for h in range(H):
        for d in range(D):
            row = 32 * (h % 4) + 16 * (h // 4) + d
            c[row, C_NUM2 + D * h + d] = 1.0
            c[row + D, C_DEN2 + D * h + d] = 1.0
    c[64:, C_STEP:C_STEP + T] = np.eye(T, dtype=f)
    t = np.arange(T)
    c[64:, C_MASK:C_MASK + T] = np.where(t[None, :] > t[:, None], f(-1e30), f(0))
    one = 0x3F80
    cb = np.zeros((P, P + 16 * T), np.uint16)
    cb[:, :P] = one * np.eye(P, dtype=np.uint16)
    for part in range(2):
        for j2 in range(16):
            cb[16 * part + j2, P + T * j2:P + T * j2 + T] = one
    return c, cb


def kernel(x, ctx_2048, L0_attn_Wq, L0_attn_bq, L0_attn_Wk, L0_attn_bk, L0_attn_Wv, L0_attn_bv, L0_attn_Wo,
           L0_attn_bo, L0_xattn_gamma, L0_ffn_w_fc, L0_ffn_w_proj):
    import numpy as np
    import concourse.bacc as bacc
    from concourse.bass_utils import run_bass_kernel_spmd
    x, ctx, wq, bq, wk, bk, wv, bv, wo, bo, gamma, wfc, wproj = (np.asarray(a) for a in (
        x, ctx_2048, L0_attn_Wq, L0_attn_bq, L0_attn_Wk, L0_attn_bk, L0_attn_Wv, L0_attn_bv, L0_attn_Wo, L0_attn_bo,
        L0_xattn_gamma, L0_ffn_w_fc, L0_ffn_w_proj))
    wq = wq.reshape(H, G, D, E).transpose(1, 0, 2, 3).reshape(E, E)
    bq = bq.reshape(H, G, D).transpose(1, 0, 2).reshape(E)
    cf, cb = constants()
    arrays = {
        "x": x.reshape(B * T, E),
        "ctxt": ctx.reshape(B * T, E),
        "ctxt_t": ctx.reshape(B * T, E).T,
        "wqkv": np.concatenate([wq, wk, wv]).T,
        "bqkv": np.concatenate([bq, bk, bv])[None],
        "wo": wo.reshape(E, H, G, D).transpose(1, 3, 2, 0).reshape(H * D, G, E),
        "bo": bo,
        "gamma": gamma.reshape(1),
        "wfc": wfc.T,
        "wproj": wproj.T,
        "cf": cf,
        "cb": cb,
    }
    nc = bacc.Bacc("TRN2", target_bir_lowering=False, num_devices=1)
    ins, args = {}, {}
    for name, a in arrays.items():
        a = np.ascontiguousarray(a)
        ins[f"in_{name}"] = a
        args[name] = nc.dram_tensor(f"in_{name}", a.shape, mybir.dt.from_np(a.dtype), kind="ExternalInput").ap()
    out = nc.dram_tensor("out_x", (B * T, E), F32, kind="ExternalOutput").ap()
    build(nc, **args, out=out)
    r = run_bass_kernel_spmd(nc, [ins], core_ids=[0])
    return r.results[0]["out_x"].reshape(B, T, E)
```

```python
from contextlib import ExitStack

import concourse.bass as bass
from concourse import mybir

ALU = mybir.AluOpType
ACT = mybir.ActivationFunctionType
AX = mybir.AxisListType
F32 = mybir.dt.float32
BF16 = mybir.dt.bfloat16
FP8 = mybir.dt.float8e4
U32 = mybir.dt.uint32
U16 = mybir.dt.uint16

P = 128
EPS = 1e-5
B, T, E = 16, 64, 256
H, G, D = 8, 4, 8
NPAIR = B // 2
SCALE = float(D) ** -0.5
F = 4 * E
KT, FT = E // P, F // P
QKV = E + 2 * H * D
FP8_MAX = 448.0
TINY = 2.0 ** -5

C_COS, C_SIN, C_HEAD, C_ID, C_NUM, C_DEN, C_STEP, C_MASK, C_NUM2, C_DEN2 = 0, 8, 16, 24, 152, 408, 664, 728, 792, 856
C_END = 920
PARTS_Q = (0, 1, 2, 0, 1, 0)
PARTS_K = (0, 0, 0, 1, 1, 2)
SPLIT = len(PARTS_Q) * D
PAIR_ROWS = 2 * SPLIT


def build(nc, x, ctxt, ctxt_t, wqkv, bqkv, wo, bo, gamma, wfc, wproj, cf, cb, out):
    with ExitStack() as stack:
        def sb(name, shape, dt=F32):
            return stack.enter_context(nc.sbuf_tensor(name, shape, dt))

        def sem(name):
            return stack.enter_context(nc.semaphore(name))

        bank = [stack.enter_context(nc.psum_tensor(f"bank{i}", [P, 512], F32)) for i in range(2)]
        ps_a = stack.enter_context(nc.psum_tensor("ps_a", [P, 2, 512], F32))
        ps_t = stack.enter_context(nc.psum_tensor("ps_t", [P, 4, 512], F32))

        x_in = sb("x_in", [P, NPAIR, E])
        xb = sb("xb", [P, NPAIR, E])
        x1 = sb("x1", [P, NPAIR, E])
        x2 = sb("x2", [P, NPAIR, E])
        ctx_t = sb("ctx_t", [P, 2, B, T])
        const = sb("const", [P, C_END])
        constb = sb("constb", [P, P + 16 * T], BF16)
        w_qkv = sb("w_qkv", [P, KT, QKV])
        b_qkv = sb("b_qkv", [1, QKV])
        ones = sb("ones", [1, P])
        w_o = sb("w_o", [P, G, E])
        bo_bc = sb("bo_bc", [P, E])
        gam = sb("gam", [P, 1])
        neg_half = sb("neg_half", [P, 1])

        wf = sb("wf", [P, KT, F])
        wp = sb("wp", [P, FT, E])

        stats = sb("stats", [P, 2, 6])
        mv = sb("mv", [P, 2, 2])
        var = sb("var", [P, 2])
        rstd = sb("rstd", [P, 2])
        xn = sb("xn", [P, 2, E])
        xn_t = sb("xn_t", [P, 2, KT, P])
        rope_c = sb("rope_c", [P, QKV - H * D])
        rope_s = sb("rope_s", [P, QKV - H * D])
        qk = sb("qk", [P, 2, QKV - H * D])
        q_t = sb("q_t", [P, 2, 2, G, T])
        k_t = sb("k_t", [H * D, 2, P])
        hid_all = sb("hid_all", [P, FT * B * T])
        hid = hid_all[:].rearrange("p (f t) -> p f t", f=FT)
        quarter = [hid_all[:, 2048 * k:2048 * k + 2048] for k in range(2)]
        k_z = quarter[0].rearrange("p (u h b t) -> p u h b t", u=2, h=H, b=2)
        v_z = sb("v_z", [P, 2, H, 32])
        nmax = sb("nmax", [P, 2, 2, H, 2])
        nmax_p = sb("nmax_p", [P, 2, 2, 2, 16], BF16)
        nmax_t = sb("nmax_t", [P, 2, 2, P], BF16)
        probs = quarter[1].rearrange("p (s c q) -> p s c q", s=2, c=4)
        u_sb = sb("u_sb", [P, 2, 2, E])
        rden = sb("rden", [P, E])
        y_t = sb("y_t", [P, 2, E])
        stats2 = sb("stats2", [P, 6])
        mv2 = sb("mv2", [P, 2])
        var2 = sb("var2", [P, 1])
        rstd2 = sb("rstd2", [P, 1])
        x1n = sb("x1n", [P, 2, E])
        rest = sb("rest", [P, 2, E])
        q_parts = sb("q_parts", [P, 2, 3, E], BF16)
        ctx_in = sb("ctx_in", [P, NPAIR, E])
        ctx_rest = sb("ctx_rest", [P, E])
        k_parts = sb("k_parts", [P, 2, 3, E], BF16)
        d_q = nc.dram_tensor("d_q", [B * 4, 2, len(PARTS_Q), D, E], BF16, kind="Internal").ap()
        d_k = nc.dram_tensor("d_k", [B * 4, 2, len(PARTS_K), D, E], BF16, kind="Internal").ap()
        q_st = sb("q_st", [P, 4, 4, E], BF16)
        k_st = hid_all[:, 4096:8192].bitcast(BF16).rearrange("p (r h a e) -> p r h a e", r=4, h=2, a=4)
        v2_z = sb("v2_z", [P, 2, 2, H, 32])
        nmax2 = sb("nmax2", [P, 2, 2, 2, 4])
        nmax2_p = sb("nmax2_p", [P, 2, 2, 2, 2, 4], BF16)
        nmax2_t = sb("nmax2_t", [16, 2, 2, P], BF16)
        probs2_all = sb("probs2", [P, 4 * 2 * 2 * E])
        probs2 = probs2_all[:].rearrange("p (r h l q) -> p r h l q", r=4, h=2, l=2)
        u2_sb = sb("u2_sb", [P, 2, E])
        rden2 = sb("rden2", [P, E])
        y2 = sb("y2", [P, E])
        stats3 = sb("stats3", [P, NPAIR, 6])
        mv3 = sb("mv3", [P, NPAIR, 2])
        var3 = sb("var3", [P, NPAIR])
        rstd3 = sb("rstd3", [P, NPAIR])
        top = sb("top", [P, 4])
        top_all = sb("top_all", [P, 4])
        unit = sb("unit", [P, 4])
        inv = sb("inv", [P, 4])
        half_inv = sb("half_inv", [P, 1])
        step1 = sb("step1", [P, 1])
        step2 = sb("step2", [P, 1])
        quant = x_in[:].rearrange("p n d -> p (n d)")
        magic = ctx_in[:].rearrange("p n d -> p (n d)")
        wf8 = sb("wf8", [P, KT, F], BF16)
        wp8 = sb("wp8", [P, 2, FT, E], BF16)
        x8 = sb("x8", [P, NPAIR, E], BF16)
        x8_t = sb("x8_t", [P, KT, B * T], BF16)
        minus_tiny = sb("minus_tiny", [P, P], BF16)
        tops = sb("tops", [P, 2 * FT])
        h_lo, h_hi = (probs2_all[:, 2048 * k:2048 * k + 2048].bitcast(FP8).rearrange("p (f t) -> p f t", f=FT) for k in range(2))
        res = x1

        sems = {}

        def s(name):
            if name not in sems:
                sems[name] = sem(name)
            return sems[name]

        names = """ld_x ld_ctx ld_small ld_w ld_wo ld_ffn setup_pool setup_dve var_ready rstd_ready xn_ready
        xt_ps xt_ready proj_ready qk_ready kt_ps qt_ps qt_ready kt_ready kz_ready v_ready
        s_ready max_done nmax_ready mt_ps mt_ready t_ready exp_done u_ready us_ready nd_ready y_ready w_ready
        x1_ready var2_ready rstd2_ready x1n_ready parts_ready chain_a chain_b chain_c chain_d chain_r chain_p passed kparts_ready max2_done nmax2_ready mt2_ps mt2_ready
        s2_ready t2_ready exp2_done pv2_done v2_ready us2_ready nd2_ready nd2_read x2_ready var3_ready rstd3_ready top_ready top_all_ready x8_ready x8t_ps x8t_ready
        wp8_ready wf8_ready fc1_ready relu_ready hid_ready hq_ready bias_ps fc2_ready res_ready stored chain_f chain_m chain_k
        """.split()
        for n in names:
            s(n)
        q_written = [sem(f"q_written{u}") for u in range(2)]
        k_written = [sem(f"k_written{u}") for u in range(2)]
        qk_loaded = [sem(f"qk_loaded{r}") for r in range(4)]
        m_loaded = [sem(f"m_loaded{r}") for r in range(4)]
        block = stack.enter_context(nc.Block())

        def wait(eng, name, value, alone=False):
            if not isinstance(value, int) or value > 0:
                eng.wait_ge(s(name) if isinstance(name, str) else name, value)
                if alone and not isinstance(value, int):
                    eng.sem_inc(s("passed"), 1)

        def steps(eng, body):
            for n in range(2):
                body(n, n)
            with eng.Fori(2, NPAIR - 3, 2) as i:
                for v in range(2):
                    body(i + v, v)
            for n in range(NPAIR - 2, NPAIR + 1):
                body(n, n % 2)

        def has(n):
            return not isinstance(n, int) or 0 <= n < NPAIR

        def steps2(eng, body):
            body(0, 0)
            with eng.Fori(1, B - 6, 4) as i:
                for v in range(4):
                    body(i + v, (1 + v) % 4)
            for n in range(B - 3, B):
                body(n, n % 4)

        def loads_of(n, r, each):
            return each // 4 * (n - r) + each

        def chained(eng, name, n, per_pair):
            done = [0]

            def link(ins, alone=False):
                done[0] += 1
                assert done[0] <= per_pair
                ins.then_inc(s(name), 1)
                wait(eng, name, n * per_pair + done[0], alone)
            return link

        tok = lambda ap: ap.rearrange("(n p) d -> p n d", p=P)

        def at(ap, n):
            return ap[:, n, :] if isinstance(n, int) else ap[:, bass.ds(n, 1), :]

        @block.sync
        def _(sp):
            sp.dma_start(x_in[:], tok(x)).then_inc(s("ld_x"), 16)
            sp.dma_start(const[:], cf).then_inc(s("ld_small"), 16)
            sp.dma_start(constb[:].bitcast(U16), cb).then_inc(s("ld_small"), 16)
            sp.dma_start(b_qkv[:], bqkv).then_inc(s("ld_small"), 16)
            sp.dma_start(w_qkv[:], wqkv.rearrange("(k p) n -> p k n", p=P)).then_inc(s("ld_w"), 16)
            sp.dma_start(bo_bc[:], bo.partition_broadcast(P)).then_inc(s("ld_wo"), 16)
            sp.dma_start(gam[:], gamma.partition_broadcast(P)).then_inc(s("ld_wo"), 16)
            for half in range(2):
                sp.dma_start(w_o[64 * half:64 * half + 64], wo).then_inc(s("ld_wo"), 16)
            sp.dma_start(wf[:], wfc.rearrange("(k p) n -> p k n", p=P)).then_inc(s("ld_ffn"), 16)
            sp.dma_start(wp[:], wproj.rearrange("(k p) n -> p k n", p=P)).then_inc(s("ld_ffn"), 16)
            sp.dma_start(ctx_in[:], tok(ctxt)).then_inc(s("ld_ctx"), 16)
            sp.dma_start(ctx_t[:], ctxt_t.rearrange("(l p) (b t) -> p l b t", p=P, t=T)).then_inc(s("ld_ctx"), 16)

            def spread(d_st, parts, src, n, written):
                rows = d_st.rearrange("(n a) h c d e -> n c (a h) d e", a=8)
                for c, part in enumerate(parts):
                    dst = rows[n, c] if isinstance(n, int) else rows[bass.ds(n, 1), c].rearrange("n a d e -> (n a) d e")
                    sp.dma_start(dst, src[:, part, :]).then_inc(written, 16)

            def load(n, r):
                q_src, k_src = (d_st[4 * n:4 * n + 4] if isinstance(n, int) else d_st[bass.ds(4 * n, 4)] for d_st in (d_q, d_k))
                sp.dma_start(q_st[0:PAIR_ROWS, r], q_src.rearrange("a h c d e -> (h c d) a e")).then_inc(qk_loaded[r], 16)
                for hp in range(2):
                    sp.dma_start(k_st[SPLIT * hp:SPLIT * hp + SPLIT, r, hp], k_src[:, hp].rearrange("a c d e -> (c d) a e")
                                 ).then_inc(qk_loaded[r], 16)

            def body(n, u):
                if isinstance(n, int) and n == NPAIR - 1:
                    for v in range(2):
                        sp.wait_ge(q_written[v], 16 * 6)
                        sp.wait_ge(k_written[v], 16 * 6)
                    sp.wait_ge(s("setup_dve"), 6)
                    for m in range(3):
                        load(m, m)
                if has(n):
                    wait(sp, "kparts_ready", n + 1)
                    spread(d_k, PARTS_K, k_parts[:, u], n, k_written[u])
                if has(n - 1):
                    wait(sp, "parts_ready", n)
                    spread(d_q, PARTS_Q, q_parts[:, 1 - u], n - 1, q_written[1 - u])
            steps(sp, body)
            for u in range(2):
                sp.wait_ge(q_written[u], 16 * 6 * 4)
                sp.wait_ge(k_written[u], 16 * 6 * 4)

            def maxima(n, r):
                wait(sp, "mt2_ready", n + 1)
                sp.dma_start(q_st[PAIR_ROWS:PAIR_ROWS + 4, r], nmax2_t[:, r % 2].rearrange("p g q -> p (g q)")
                             ).then_inc(m_loaded[r], 16)

            maxima(0, 0)

            def body2(n, r):
                if not isinstance(n, int) or n + 1 < B:
                    maxima(n + 1, (r + 1) % 4)
                if not isinstance(n, int) or n + 3 < B:
                    wait(sp, "t2_ready", 4 * n)
                    load(n + 3, (r + 3) % 4)
            steps2(sp, body2)
            for n in range(NPAIR):
                sp.wait_ge(s("res_ready"), n + 1)
                sp.dma_start(tok(out)[:, n, :], res[:, n, :]).then_inc(s("stored"), 16)
            sp.wait_ge(s("stored"), 16 * NPAIR)

        @block.gpsimd
        def _(pool):
            nc.gpsimd.memset(ones[:], 1.0).then_inc(s("setup_pool"), 1)
            nc.gpsimd.memset(neg_half[:], -0.5).then_inc(s("setup_pool"), 1)
            nc.gpsimd.memset(nmax_t[:], 0.0).then_inc(s("setup_pool"), 1)
            for u in range(2):
                nc.gpsimd.memset(v_z[:, u], 0.0).then_inc(s("setup_pool"), 1)
            pool.wait_ge(s("setup_pool"), 5)
            for u in range(2):
                nc.gpsimd.memset(v_z[0:64, u, :, 8:16], 1.0).then_inc(s("setup_pool"), 1)
            for u in range(2):
                pool.wait_ge(s("setup_pool"), 7 + u)
                nc.gpsimd.memset(v_z[64:128, u, :, 24:32], 1.0).then_inc(s("setup_pool"), 1)
            pool.wait_ge(s("ld_small"), 48)
            pool.wait_ge(s("setup_pool"), 9)
            for u in range(2):
                nc.gpsimd.tensor_copy(q_t[64:128, u].rearrange("p b g t -> p (b g) t"),
                                      const[64:128, C_STEP:C_STEP + T].unsqueeze(1).to_broadcast([64, 2 * G, T])
                                      ).then_inc(s("setup_pool"), 1)
                nc.gpsimd.tensor_copy(k_z[64:128, u].rearrange("p h b t -> p (h b) t"),
                                      const[64:128, C_MASK:C_MASK + T].unsqueeze(1).to_broadcast([64, 2 * H, T])
                                      ).then_inc(s("setup_pool"), 1)
            pool.wait_ge(s("setup_pool"), 13)
            nc.gpsimd.memset(v2_z[:], 0.0).then_inc(s("setup_pool"), 1)
            pool.wait_ge(s("setup_pool"), 14)
            for hh in range(2):
                for u in range(2):
                    nc.gpsimd.memset(v2_z[:, u, :, 4 * hh:4 * hh + 4, 16 * hh + 8:16 * hh + 16], 1.0).then_inc(s("setup_pool"), 1)
            
            def rstd_a(n, u):
                wait(pool, "var_ready", n + 1)
                nc.gpsimd.tensor_tensor(rstd[:, u:u + 1], var[:, u:u + 1], neg_half[:], ALU.pow).then_inc(s("rstd_ready"), 1)

            def heads_a(n, u):
                wait(pool, "kt_ready", n + 1)
                wait(pool, "t_ready", 2 * (n - 1))
                nc.gpsimd.tensor_tensor(
                    k_z[0:64, u].rearrange("p h b t -> p h (b t)"),
                    k_t[:, u, :].unsqueeze(1).to_broadcast([64, H, P]),
                    const[0:64, C_HEAD:C_HEAD + H].unsqueeze(2).to_broadcast([64, H, P]), ALU.mult).then_inc(s("kz_ready"), 1)

            def rstd_c(n, u):
                wait(pool, "var2_ready", n + 1)
                nc.gpsimd.tensor_tensor(rstd2[:], var2[:], neg_half[:], ALU.pow).then_inc(s("rstd2_ready"), 1)

            def parts_c(n, u):
                link = chained(pool, "chain_p", n, 3)
                wait(pool, "x1n_ready", n + 1)
                wait(pool, q_written[u], 48 * (n - u), alone=True)
                link(nc.gpsimd.tensor_copy(q_parts[:, u, 0, :], x1n[:, u, :]))
                link(nc.gpsimd.tensor_tensor(rest[:, u, :], x1n[:, u, :], q_parts[:, u, 0, :], ALU.subtract), alone=True)
                link(nc.gpsimd.tensor_copy(q_parts[:, u, 1, :], rest[:, u, :]))
                nc.gpsimd.tensor_tensor(q_parts[:, u, 2, :], rest[:, u, :], q_parts[:, u, 1, :], ALU.subtract).then_inc(s("parts_ready"), 1)

            def context(n, u):
                link = chained(pool, "chain_k", n, 3)
                wait(pool, k_written[u], 48 * (n - u), alone=True)
                c_n = at(ctx_in, n)
                k0, k1, k2 = (k_parts[:, u, c, :] if isinstance(n, int) else k_parts[:, u, c:c + 1, :] for c in range(3))
                r_n = ctx_rest[:] if isinstance(n, int) else ctx_rest[:].unsqueeze(1)
                link(nc.gpsimd.tensor_copy(k0, c_n), alone=True)
                link(nc.gpsimd.tensor_tensor(r_n, c_n, k0, ALU.subtract), alone=True)
                link(nc.gpsimd.tensor_copy(k1, r_n), alone=True)
                nc.gpsimd.tensor_tensor(k2, r_n, k1, ALU.subtract).then_inc(s("kparts_ready"), 1)

            def body(n, u):
                if has(n + 1):
                    heads_a(n + 1, 1 - u)
                if has(n - 1):
                    rstd_c(n - 1, 1 - u)
                if has(n + 2):
                    rstd_a(n + 2, u)
                if has(n - 1):
                    parts_c(n - 1, 1 - u)
                if has(n):
                    context(n, u)

            rstd_a(0, 0)
            rstd_a(1, 1)
            pool.wait_ge(s("ld_wo"), 64)
            nc.gpsimd.tensor_tensor(xb[:], x_in[:], bo_bc[:].unsqueeze(1).to_broadcast([P, NPAIR, E]), ALU.add).then_inc(s("setup_pool"), 1)
            heads_a(0, 0)
            pool.wait_ge(s("ld_ctx"), 32)
            steps(pool, body)

            def values(n, u):
                wait(pool, "pv2_done", 2 * (n - 1))
                for hh in range(2):
                    src = ctx_t[:, :, n, 32 * hh:32 * hh + 32] if isinstance(n, int) else ctx_t[:, :, bass.ds(n, 1), 32 * hh:32 * hh + 32].rearrange("p l n d -> p l (n d)")
                    ins = nc.gpsimd.tensor_copy(v2_z[:, u, :, 4 * hh:4 * hh + 4, 16 * hh:16 * hh + D], src.rearrange("p l (c d) -> p l c d", d=D))
                ins.then_inc(s("v2_ready"), 1)

            values(0, 0)
            values(1, 1)

            def body2(n, r):
                if not isinstance(n, int) or n + 2 < B:
                    values(n + 2, r % 2)
            steps2(pool, body2)

            nc.gpsimd.memset(minus_tiny[:], -TINY).then_inc(s("setup_pool"), 1)
            for k in range(4):
                if k == 2:
                    pool.wait_ge(s("var3_ready"), 1)
                    nc.gpsimd.tensor_tensor(rstd3[:], var3[:], neg_half[:].to_broadcast([P, NPAIR]), ALU.pow).then_inc(s("rstd3_ready"), 1)
                pool.wait_ge(s("top_ready"), k + 1)
                nc.gpsimd.partition_all_reduce(top_all[:, k:k + 1], top[:, k:k + 1], P, bass.bass_isa.ReduceOp.max
                                               ).then_inc(s("top_all_ready"), 1)

        @block.tensor
        def _(pe):
            ident = const[:, C_ID:C_ID + P]
            pe.wait_ge(s("ld_small"), 48)
            pe.wait_ge(s("ld_w"), 16)
            pe.wait_ge(s("setup_pool"), 13)
            pe.wait_ge(s("ld_wo"), 64)

            def turn_x(n, u):
                wait(pe, "xn_ready", n + 1)
                wait(pe, "kt_ready", n)
                for k in range(KT):
                    mm = nc.tensor.transpose(bank[0][:, P * k:P * k + P], xn[:, u, P * k:P * k + P], ident)
                mm.then_inc(s("xt_ps"), 1)

            def project(n, u):
                wait(pe, "xt_ready", n + 1)
                wait(pe, "v_ready", n)
                nc.tensor.matmul(bank[1][:, 0:QKV], ones[:], b_qkv[:], start=True, stop=False)
                for k in range(KT):
                    mm = nc.tensor.matmul(bank[1][:, 0:QKV], xn_t[:, u, k, :], w_qkv[:, k, :], start=False, stop=(k == KT - 1))
                mm.then_inc(s("proj_ready"), 1)

            def turn_qk(n, u):
                wait(pe, "qk_ready", n + 1)
                wait(pe, "qt_ready", n, alone=True)
                nc.tensor.transpose(bank[0][0:64, 2 * P:3 * P], qk[:, u, E:E + 64], ident).then_inc(s("kt_ps"), 1)
                for g in range(G):
                    mm = nc.tensor.transpose(ps_a[0:64, 0, P * g:P * g + P], qk[:, u, 64 * g:64 * g + 64], ident)
                mm.then_inc(s("qt_ps"), 1)

            def scores_q(n, u, k):
                b, gp = k // 2, k % 2
                if k == 0:
                    wait(pe, "qt_ready", n + 1)
                    wait(pe, "kz_ready", n + 1)
                if k == 1:
                    wait(pe, "x1_ready", n - 1)
                if k >= 2:
                    wait(pe, "max_done", 4 * n + k - 1)
                nc.tensor.matmul(ps_t[:, 2 + k % 2, :], q_t[:, u, b, 2 * gp:2 * gp + 2, :].rearrange("p g t -> p (g t)"),
                                 k_z[:, u, :, b, :], start=True, stop=True).then_inc(s("s_ready"), 1)

            def turn_nmax(n, u):
                wait(pe, "nmax_ready", n + 1)
                pst = ps_t[0:32, 2, 0:P].bitcast(BF16)
                for gp in range(2):
                    mm = nc.tensor.transpose(pst[:, P * gp:P * gp + P], nmax_p[:, u, gp].rearrange("p a b -> p (a b)"), constb[:, 0:P])
                mm.then_inc(s("mt_ps"), 1)

            def scores_k(n, u, hh):
                if hh == 0:
                    wait(pe, "mt_ready", n + 1)
                wait(pe, "exp_done", 2 * n + hh)
                for c in range(4):
                    for b in range(2):
                        h = 4 * hh + c
                        o = ps_t[64 * b:64 * b + 64, c // 2, E * (c % 2):E * (c % 2) + E]
                        nc.tensor.matmul(o, k_z[:, u, h, b, :], q_t[:, u, b].rearrange("p g t -> p (g t)"),
                                         start=True, stop=False)
                        j = 2 * h + b
                        mm = nc.tensor.matmul(o, constb[:, P + T * j:P + T * j + T],
                                              nmax_t[:, u].rearrange("p g q -> p (g q)"), start=False, stop=True)
                mm.then_inc(s("t_ready"), 1)

            def weigh_v(n, u, hh):
                if hh == 0:
                    wait(pe, "v_ready", n + 1)
                wait(pe, "exp_done", 2 * n + hh + 1)
                for c in range(4):
                    mm = nc.tensor.matmul(ps_a[32 * c:32 * c + 32, 1, E * hh:E * hh + E], v_z[:, u, 4 * hh + c, :],
                                          probs[:, hh, c, :], start=True, stop=True)
                if hh == 1:
                    mm.then_inc(s("u_ready"), 1)

            def sort_heads(n, u):
                wait(pe, "us_ready", n + 1)
                for k, col in enumerate((C_DEN, C_NUM)):
                    for hh in range(2):
                        mm = nc.tensor.matmul(ps_a[:, 1, E * k:E * k + E], const[:, col + P * hh:col + P * hh + P],
                                              u_sb[:, u, hh, :], start=(hh == 0), stop=(hh == 1))
                mm.then_inc(s("nd_ready"), 1)

            def project_out(n, u):
                wait(pe, "y_ready", n + 1, alone=True)
                for g in range(G):
                    for b in range(2):
                        r = slice(64 * b, 64 * b + 64)
                        mm = nc.tensor.matmul(ps_t[r, 3, 0:E], y_t[r, u, T * g:T * g + T], w_o[r, g, :],
                                              start=(g == 0), stop=(g == G - 1))
                mm.then_inc(s("w_ready"), 1)

            def scores(n, r, ht):
                if ht == 0:
                    wait(pe, qk_loaded[r], loads_of(n, r, 48))
                for hp in range(2):
                    wait(pe, "max2_done", 8 * n + 2 * ht + hp - 1)
                    for half in range(2):
                        mm = nc.tensor.matmul(bank[hp][:, E * half:E * half + E], q_st[0:PAIR_ROWS, r, ht, P * half:P * half + P],
                                              k_st[0:PAIR_ROWS, r, hp, ht, :], start=True, stop=True)
                    mm.then_inc(s("s2_ready"), 1)

            def turn_maxima(n, r):
                wait(pe, "nmax2_ready", n + 1)
                wait(pe, "nd2_read", n - 1 - r % 2)
                dst = ps_a[0:16, 1, 0:P].bitcast(BF16)
                for half in range(2):
                    mm = nc.tensor.transpose(dst[:, P * half:P * half + P],
                                             nmax2_p[:, r % 2, half].rearrange("p h c t -> p (h c t)"), constb[:, 0:P])
                mm.then_inc(s("mt2_ps"), 1)

            def scores_t(n, r, ht):
                if ht == 0:
                    wait(pe, m_loaded[r], loads_of(n, r, 16))
                wait(pe, "exp2_done", 4 * n + ht - 1)
                for hp in range(2):
                    for half in range(2):
                        mm = nc.tensor.matmul(ps_t[:, 2 * (ht % 2) + hp, E * half:E * half + E],
                                              k_st[:, r, hp, ht, P * half:P * half + P], q_st[:, r, ht, :], start=True, stop=True)
                mm.then_inc(s("t2_ready"), 1)

            def weigh(n, r, hh):
                b = r % 2
                wait(pe, "exp2_done", 4 * n + 2 * hh + 2)
                if hh == 0:
                    wait(pe, "v2_ready", n + 1)
                    if b == 0:
                        wait(pe, "us2_ready", n)
                for half in range(2):
                    for c in range(4):
                        mm = nc.tensor.matmul(ps_a[32 * c:32 * c + 32, 0, E * b:E * b + E], v2_z[:, b, half, 4 * hh + c, :],
                                              probs2[:, 2 * hh + c // 2, c % 2, half, :],
                                              start=(b == 0 and hh == 0 and half == 0), stop=(hh == 1 and half == 1),
                                              skip_group_check=True)
                mm.then_inc(s("pv2_done"), 1)

            def gather_heads(n):
                wait(pe, "us2_ready", n)
                wait(pe, "mt2_ready", n + 2 if not isinstance(n, int) else min(n + 2, B))
                wait(pe, "nd2_read", n - 1)
                for k, col in enumerate((C_NUM2, C_DEN2)):
                    for b in range(2):
                        mm = nc.tensor.matmul(ps_a[64 * b:64 * b + 64, 1, E * k:E * k + E], const[:, col:col + 64],
                                              u2_sb[:, b, :], start=True, stop=True)
                    mm.then_inc(s("nd2_ready"), 1)

            turn_x(0, 0)
            project(0, 0)
            turn_qk(0, 0)

            def body(n, u):
                if has(n):
                    scores_q(n, u, 0)
                if has(n - 1):
                    weigh_v(n - 1, 1 - u, 1)
                last = isinstance(n, int) and n == NPAIR
                if last:
                    scores(0, 0, 0)
                    scores(0, 0, 1)
                if has(n):
                    for k in range(1, 4):
                        scores_q(n, u, k)
                if has(n + 1):
                    turn_x(n + 1, 1 - u)
                if has(n - 1):
                    sort_heads(n - 1, 1 - u)
                if last:
                    scores(0, 0, 2)
                    scores(0, 0, 3)
                if has(n):
                    turn_nmax(n, u)
                if has(n + 1):
                    project(n + 1, 1 - u)
                if has(n):
                    scores_k(n, u, 0)
                if has(n + 1):
                    turn_qk(n + 1, 1 - u)
                if has(n - 1):
                    project_out(n - 1, 1 - u)
                if has(n):
                    scores_k(n, u, 1)
                    weigh_v(n, u, 0)
            steps(pe, body)

            pe.wait_ge(s("x1_ready"), NPAIR)
            pe.sem_inc(s("nd2_ready"), 1)
            for ht in range(4):
                scores(1, 1, ht)
            turn_maxima(0, 0)

            def body2(n, r):
                known = isinstance(n, int)
                ahead = not known or n + 2 < B
                if ahead:
                    scores(n + 2, (r + 2) % 4, 0)
                scores_t(n, r, 0)
                if not known or n + 1 < B:
                    turn_maxima(n + 1, (r + 1) % 4)
                if not known or n > 0:
                    weigh(n - 1, (r - 1) % 4, 1)
                if ahead:
                    scores(n + 2, (r + 2) % 4, 1)
                scores_t(n, r, 1)
                if ahead:
                    scores(n + 2, (r + 2) % 4, 2)
                scores_t(n, r, 2)
                if r % 2 == 0 and (not known or n > 0):
                    gather_heads(n)
                weigh(n, r, 0)
                if ahead:
                    scores(n + 2, (r + 2) % 4, 3)
                scores_t(n, r, 3)
            steps2(pe, body2)
            weigh(B - 1, 3, 1)
            gather_heads(B)

            pe.wait_ge(s("x2_ready"), NPAIR)
            pe.wait_ge(s("setup_pool"), 20)
            for n in range(NPAIR):
                pe.wait_ge(s("x8_ready"), 1)
                for k in range(KT):
                    mm = nc.tensor.transpose(bank[k][:].bitcast(BF16)[:, P * n:P * n + P], x8[:, n, P * k:P * k + P], constb[:, 0:P])
            mm.then_inc(s("x8t_ps"), 1)
            pe.wait_ge(s("wp8_ready"), 1)
            for f in range(FT):
                mm = nc.tensor.matmul(ps_a[:, 0, 0:E], minus_tiny[:], wp8[:, 0, f, :], start=(f == 0), stop=(f == FT - 1))
            mm.then_inc(s("bias_ps"), 1)
            pe.wait_ge(s("wf8_ready"), 1)
            pe.wait_ge(s("x8t_ready"), 2)
            for i in range(2 * FT):
                f, half = i // 2, i % 2
                if i >= 4:
                    pe.wait_ge(s("relu_ready"), i - 3)
                for k in range(KT):
                    mm = nc.tensor.matmul(ps_t[:, i % 4, :], wf8[:, k, P * f:P * f + P], x8_t[:, k, 512 * half:512 * half + 512],
                                          start=(k == 0), stop=(k == KT - 1))
                mm.then_inc(s("fc1_ready"), 1)
            pe.wait_ge(s("relu_ready"), 2 * FT)
            for n in range(NPAIR):
                pe.wait_ge(s("hq_ready"), 2 * (n // 4 + 1))
                if n >= 4:
                    pe.wait_ge(s("res_ready"), n - 3)
                for part, h8 in enumerate((h_lo, h_hi)):
                    for f in range(FT):
                        mm = nc.tensor.matmul(ps_t[:, n % 4, 0:E], h8[:, f, P * n:P * n + P], wp8[:, part, f, :],
                                              start=(part == 0 and f == 0), stop=(part == 1 and f == FT - 1))
                mm.then_inc(s("fc2_ready"), 1)

        @block.scalar
        def _(act):
            def keep_x(n, u):
                wait(act, "xt_ps", n + 1)
                nc.scalar.copy(xn_t[:, u].rearrange("p k t -> p (k t)"), bank[0][:, 0:2 * P]).then_inc(s("xt_ready"), 1)

            def keep_v(n, u):
                wait(act, "qk_ready", n + 1)
                wait(act, "u_ready", n - 1)
                for b in range(2):
                    r = slice(64 * b, 64 * b + 64)
                    ins = nc.scalar.copy(v_z[r, u, :, 16 * b:16 * b + D],
                                         bank[1][r, E + 64:QKV].rearrange("p (h d) -> p h d", d=D))
                ins.then_inc(s("v_ready"), 1)

            def keep_qk(n, u):
                wait(act, "kt_ps", n + 1)
                nc.scalar.copy(k_t[:, u, :], bank[0][0:64, 2 * P:3 * P]).then_inc(s("kt_ready"), 1)
                wait(act, "qt_ps", n + 1)
                wait(act, "t_ready", 2 * (n - 1))
                for b in range(2):
                    ins = nc.scalar.copy(q_t[0:64, u, b], ps_a[0:64, 0, :].rearrange("p (g b t) -> p b g t", b=2, t=T)[:, b])
                ins.then_inc(s("qt_ready"), 1)

            def keep_nmax(n, u):
                wait(act, "mt_ps", n + 1)
                nc.scalar.copy(nmax_t[0:32, u].rearrange("p g q -> p (g q)"), ps_t[0:32, 2, 0:P].bitcast(BF16)).then_inc(s("mt_ready"), 1)

            def exp(n, hh):
                wait(act, "t_ready", 2 * n + hh + 1)
                nc.scalar.activation(probs[:, hh].rearrange("p c q -> p (c q)"),
                                     ps_t[:, 0:2, :].rearrange("p a b -> p (a b)"), ACT.Exp, scale=SCALE).then_inc(s("exp_done"), 1)

            def keep_sums_a(n, u):
                wait(act, "u_ready", n + 1)
                nc.scalar.copy(u_sb[:, u].rearrange("p b q -> p (b q)"), ps_a[:, 1, :]).then_inc(s("us_ready"), 1)

            keep_x(0, 0)
            keep_v(0, 0)
            keep_qk(0, 0)

            def body(n, u):
                if has(n - 1):
                    keep_sums_a(n - 1, 1 - u)
                if has(n + 1):
                    keep_x(n + 1, 1 - u)
                if has(n):
                    keep_nmax(n, u)
                if has(n + 1):
                    keep_v(n + 1, 1 - u)
                if has(n):
                    exp(n, 0)
                if has(n + 1):
                    keep_qk(n + 1, 1 - u)
                if has(n):
                    exp(n, 1)
            steps(act, body)

            def exp2(n, r, ht):
                wait(act, "t2_ready", 4 * n + ht + 1)
                wait(act, "pv2_done", 2 * (n - 1) + ht // 2 + 1)
                b = 2 * (ht % 2)
                nc.scalar.activation(probs2[:, ht].rearrange("p h l q -> p (h l q)"),
                                     ps_t[:, b:b + 2, :].rearrange("p a b -> p (a b)"), ACT.Exp, scale=SCALE).then_inc(s("exp2_done"), 1)

            def keep_maxima(n, r):
                wait(act, "mt2_ps", n + 1)
                nc.scalar.copy(nmax2_t[:, r % 2].rearrange("p g q -> p (g q)"), ps_a[0:16, 1, 0:P].bitcast(BF16)).then_inc(s("mt2_ready"), 1)

            def keep_sums(n):
                wait(act, "pv2_done", 2 * n)
                wait(act, "nd2_ready", n - 1)
                for b in range(2):
                    nc.scalar.copy(u2_sb[:, b, :], ps_a[:, 0, E * b:E * b + E]).then_inc(s("us2_ready"), 1)

            keep_maxima(0, 0)

            def body2(n, r):
                known = isinstance(n, int)
                exp2(n, r, 0)
                if not known or n + 1 < B:
                    keep_maxima(n + 1, (r + 1) % 4)
                if r % 2 == 0 and (not known or n > 0):
                    keep_sums(n)
                exp2(n, r, 1)
                exp2(n, r, 2)
                exp2(n, r, 3)
            steps2(act, body2)
            keep_sums(B)

            act.wait_ge(s("x8t_ps"), 1)
            for k in range(KT):
                nc.scalar.copy(x8_t[:, k, :], bank[k][:].bitcast(BF16)).then_inc(s("x8t_ready"), 1)
            for i in range(2 * FT):
                f, half = i // 2, i % 2
                part = hid[:, f, 512 * half:512 * half + 512]
                act.wait_ge(s("relu_ready"), i + 1)
                nc.scalar.activation(part, part, ACT.Square, scale=step1[:, 0:1]).then_inc(s("hid_ready"), 1)

        @block.vector
        def _(dve):
            NQ = QKV - H * D

            def norm_a(n, u):
                link = chained(dve, "chain_a", n, 2)
                link(nc.vector.bn_stats(stats[:, u, :], at(x_in, n)), alone=True)
                link(nc.vector.bn_aggr(mv[:, u, :], stats[:, u, :]), alone=True)
                nc.vector.tensor_scalar(var[:, u:u + 1], mv[:, u, 1:2], EPS, None, ALU.add).then_inc(s("var_ready"), 1)

            def apply_a(n, u):
                wait(dve, "rstd_ready", n + 1)
                nc.vector.tensor_scalar(xn[:, u, :], at(x_in, n), mv[:, u, 0:1], rstd[:, u:u + 1], ALU.subtract, ALU.mult).then_inc(s("xn_ready"), 1)

            def rotate(n, u):
                link = chained(dve, "chain_r", n, 3)
                wait(dve, "proj_ready", n + 1)
                heads = bank[1][:, 0:NQ].rearrange("p (a d) -> p a d", d=D)
                sh = rope_s[:].rearrange("p (a d) -> p a d", d=D)
                nc.vector.tensor_tensor(rope_c[:].rearrange("p (a d) -> p a d", d=D), heads,
                                        const[:, C_COS:C_COS + D].unsqueeze(1).to_broadcast([P, NQ // D, D]), ALU.mult).then_inc(s("chain_r"), 1)
                nc.vector.tensor_tensor(sh[:, :, 0:4], heads[:, :, 4:8],
                                        const[:, C_SIN:C_SIN + 4].unsqueeze(1).to_broadcast([P, NQ // D, 4]), ALU.mult).then_inc(s("chain_r"), 1)
                nc.vector.tensor_tensor(sh[:, :, 4:8], heads[:, :, 0:4],
                                        const[:, C_SIN + 4:C_SIN + 8].unsqueeze(1).to_broadcast([P, NQ // D, 4]), ALU.mult).then_inc(s("chain_r"), 1)
                wait(dve, "chain_r", 3 * n + 3)
                nc.vector.tensor_tensor(qk[:, u, :], rope_c[:], rope_s[:], ALU.add).then_inc(s("qk_ready"), 1)

            def maxima_a(n, u):
                link = chained(dve, "chain_b", n, 1)
                for k in range(4):
                    b, gp = k // 2, k % 2
                    wait(dve, "s_ready", 4 * n + k + 1)
                    nc.vector.tensor_reduce(nmax[:, u, gp, :, b], ps_t[:, 2 + k % 2, :].rearrange("p (h t) -> p h t", t=T), AX.X, ALU.max,
                                            negate=True).then_inc(s("max_done"), 1)
                wait(dve, "max_done", 4 * n + 4)
                flat = nmax[:, u].rearrange("p g h b -> p g (h b)")
                link(nc.vector.tensor_copy(nmax_p[:, u, :, 0, :], flat))
                nc.vector.tensor_tensor(nmax_p[:, u, :, 1, :], flat, nmax_p[:, u, :, 0, :], ALU.subtract).then_inc(s("nmax_ready"), 1)

            def divide(n, u):
                link = chained(dve, "chain_d", n, 1)
                wait(dve, "nd_ready", n + 1)
                link(nc.vector.reciprocal(rden[:], ps_a[:, 1, 0:E]))
                nc.vector.tensor_tensor(y_t[:, u, :], ps_a[:, 1, E:2 * E], rden[:], ALU.mult).then_inc(s("y_ready"), 1)

            def norm_c(n):
                link = chained(dve, "chain_c", n, 2)
                wait(dve, "w_ready", n + 1)
                x1_n = at(x1, n)
                nc.vector.tensor_tensor(x1_n, ps_t[:, 3, 0:E] if isinstance(n, int) else ps_t[:, 3:4, 0:E], at(xb, n), ALU.add).then_inc(s("x1_ready"), 1)
                wait(dve, "x1_ready", n + 1, alone=True)
                link(nc.vector.bn_stats(stats2[:], x1_n), alone=True)
                link(nc.vector.bn_aggr(mv2[:], stats2[:]))
                nc.vector.tensor_scalar(var2[:], mv2[:, 1:2], EPS, None, ALU.add).then_inc(s("var2_ready"), 1)

            def apply_c(n, u):
                wait(dve, "rstd2_ready", n + 1)
                wait(dve, "parts_ready", n - 1)
                nc.vector.tensor_scalar(x1n[:, u, :] if isinstance(n, int) else x1n[:, u:u + 1, :], at(x1, n), mv2[:, 0:1], rstd2[:],
                                        ALU.subtract, ALU.mult).then_inc(s("x1n_ready"), 1)

            def maxima(n, r, ht):
                for hp in range(2):
                    wait(dve, "s2_ready", 8 * n + 2 * ht + hp + 1)
                    nc.vector.tensor_reduce(nmax2[:, r % 2, :, hp, ht], bank[hp][:].rearrange("p (a k) -> p a k", k=E), AX.X, ALU.max,
                                            negate=True).then_inc(s("max2_done"), 1)

            def split_maxima(n, r):
                link = chained(dve, "chain_m", n, 1)
                wait(dve, "max2_done", 8 * n + 8)
                wait(dve, "mt2_ps", n - 1)
                link(nc.vector.tensor_copy(nmax2_p[:, r % 2, :, :, 0, :], nmax2[:, r % 2]))
                nc.vector.tensor_tensor(nmax2_p[:, r % 2, :, :, 1, :], nmax2[:, r % 2], nmax2_p[:, r % 2, :, :, 0, :], ALU.subtract).then_inc(s("nmax2_ready"), 1)

            nc.vector.memset(k_st[:, 0:2], 0.0).then_inc(s("setup_dve"), 1)
            nc.vector.memset(k_st[:, 2:4], 0.0).then_inc(s("setup_dve"), 1)
            nc.vector.memset(q_st[PAIR_ROWS:P], 0.0).then_inc(s("setup_dve"), 1)
            dve.wait_ge(s("setup_dve"), 3)
            nc.vector.memset(k_st[PAIR_ROWS:PAIR_ROWS + 4, :, 1], 1.0).then_inc(s("setup_dve"), 1)
            dve.wait_ge(s("setup_dve"), 4)
            nc.vector.memset(k_st[PAIR_ROWS:PAIR_ROWS + 2, :, 1], 0.0).then_inc(s("setup_dve"), 1)
            nc.vector.memset(k_st[PAIR_ROWS:PAIR_ROWS + 2, :, 0], 1.0).then_inc(s("setup_dve"), 1)
            dve.wait_ge(s("ld_x"), 16)
            dve.wait_ge(s("ld_small"), 48)
            norm_a(0, 0)
            norm_a(1, 1)
            apply_a(0, 0)
            apply_a(1, 1)
            rotate(0, 0)
            dve.wait_ge(s("setup_pool"), 19)

            def body(n, u):
                last = isinstance(n, int) and n == NPAIR
                if has(n):
                    maxima_a(n, u)
                if last:
                    maxima(0, 0, 0)
                    maxima(0, 0, 1)
                if has(n - 1):
                    divide(n - 1, 1 - u)
                if last:
                    maxima(0, 0, 2)
                    maxima(0, 0, 3)
                if has(n + 1):
                    rotate(n + 1, 1 - u)
                if has(n - 1):
                    norm_c(n - 1)
                if has(n + 2):
                    norm_a(n + 2, u)
                if has(n - 1):
                    apply_c(n - 1, 1 - u)
                if has(n + 2):
                    apply_a(n + 2, u)
            steps(dve, body)

            def finish(n):
                known = isinstance(n, int)
                cols = slice(P * (n - 2), P * n) if known else bass.ds(P * (n - 2), 2 * P)
                flat = [a[:].rearrange("p n d -> p (n d)")[:, cols] for a in (x1, x2)]
                wait(dve, "nd2_ready", n + 1)
                nc.vector.reciprocal(rden2[:], ps_a[:, 1, E:2 * E]).then_inc(s("nd2_read"), 1)
                wait(dve, "nd2_read", n)
                nc.vector.tensor_tensor(y2[:], ps_a[:, 1, 0:E], rden2[:], ALU.mult).then_inc(s("nd2_read"), 1)
                wait(dve, "nd2_read", n + 1)
                nc.vector.scalar_tensor_tensor(out=flat[1], in0=y2[:], scalar=gam[:, 0:1], in1=flat[0], op0=ALU.mult, op1=ALU.add
                                               ).then_inc(s("x2_ready"), 1)

            dve.sem_inc(s("nd2_read"), 1)
            split_maxima(0, 0)
            for ht in range(4):
                maxima(1, 1, ht)
            split_maxima(1, 1)

            def body2(n, r):
                known = isinstance(n, int)
                ahead = not known or n + 2 < B
                if ahead:
                    for ht in range(3):
                        maxima(n + 2, (r + 2) % 4, ht)
                if r % 2 == 0 and (not known or n > 0):
                    finish(n)
                if ahead:
                    maxima(n + 2, (r + 2) % 4, 3)
                    split_maxima(n + 2, (r + 2) % 4)
            steps2(dve, body2)
            finish(B)

            link = chained(dve, "chain_f", 0, 100)

            def scale_of(k):
                dve.wait_ge(s("top_all_ready"), k + 1)
                link(nc.vector.tensor_scalar(unit[:, k:k + 1], top_all[:, k:k + 1], 1.0 / FP8_MAX, 1e-6, ALU.mult, ALU.max))
                link(nc.vector.reciprocal(inv[:, k:k + 1], unit[:, k:k + 1]))

            def round_fp8(dst, src, k):
                link(nc.vector.tensor_scalar(quant, src, inv[:, k:k + 1], None, ALU.mult))
                link(nc.vector.tensor_scalar(magic.bitcast(U32), quant.bitcast(U32), 0x7F800000, None, ALU.bitwise_and))
                link(nc.vector.tensor_scalar(magic, magic, 2.0 ** -6, 1.5 * 2.0 ** 20, ALU.max, ALU.mult))
                link(nc.vector.tensor_tensor(quant, quant, magic, ALU.add))
                return nc.vector.tensor_tensor(dst, quant, magic, ALU.subtract)

            dve.wait_ge(s("ld_ffn"), 32)
            for k, w in enumerate((wf, wp)):
                nc.vector.tensor_reduce(top[:, k:k + 1], w[:].rearrange("p k n -> p (k n)"), AX.X, ALU.max, apply_absolute_value=True
                                        ).then_inc(s("top_ready"), 1)
            scale_of(0)
            round_fp8(wf8[:].rearrange("p k n -> p (k n)"), wf[:].rearrange("p k n -> p (k n)"), 0).then_inc(s("wf8_ready"), 1)
            dve.wait_ge(s("wf8_ready"), 1)
            scale_of(1)
            link(round_fp8(wp8[:, 0].rearrange("p k n -> p (k n)"), wp[:].rearrange("p k n -> p (k n)"), 1))
            nc.vector.tensor_scalar(wp8[:, 1], wp8[:, 0], 2.0, None, ALU.mult).then_inc(s("wp8_ready"), 1)
            dve.wait_ge(s("x2_ready"), NPAIR)
            for n in range(NPAIR):
                ins = nc.vector.bn_stats(stats3[:, n, :], x2[:, n, :])
            link(ins)
            for n in range(NPAIR):
                ins = nc.vector.bn_aggr(mv3[:, n, :], stats3[:, n, :])
            link(ins)
            nc.vector.tensor_scalar(var3[:], mv3[:, :, 1], EPS, None, ALU.add).then_inc(s("var3_ready"), 1)
            dve.wait_ge(s("rstd3_ready"), 1)
            for n in range(NPAIR):
                ins = nc.vector.tensor_scalar(xb[:, n, :], x2[:, n, :], mv3[:, n, 0:1], rstd3[:, n:n + 1], ALU.subtract, ALU.mult)
            link(ins)
            xn_all = xb[:].rearrange("p n d -> p (n d)")
            nc.vector.tensor_reduce(top[:, 2:3], xn_all, AX.X, ALU.max, apply_absolute_value=True).then_inc(s("top_ready"), 1)
            scale_of(2)
            link(nc.vector.tensor_tensor(step1[:], unit[:, 0:1], unit[:, 2:3], ALU.mult))
            round_fp8(x8[:].rearrange("p n d -> p (n d)"), xn_all, 2).then_inc(s("x8_ready"), 1)
            for i in range(2 * FT):
                f, half = i // 2, i % 2
                dve.wait_ge(s("fc1_ready"), i + 1)
                nc.vector.tensor_scalar(hid[:, f, 512 * half:512 * half + 512], ps_t[:, i % 4, :], 0.0, None, ALU.max, ALU.max,
                                        accum_out=tops[:, i:i + 1]).then_inc(s("relu_ready"), 1)
            dve.wait_ge(s("relu_ready"), 2 * FT)
            link(nc.vector.tensor_reduce(top[:, 3:4], tops[:], AX.X, ALU.max))
            link(nc.vector.tensor_tensor(top[:, 3:4], top[:, 3:4], step1[:], ALU.mult))
            nc.vector.tensor_tensor(top[:, 3:4], top[:, 3:4], top[:, 3:4], ALU.mult).then_inc(s("top_ready"), 1)
            scale_of(3)
            link(nc.vector.tensor_scalar(half_inv[:], inv[:, 3:4], 0.5, None, ALU.mult))
            link(nc.vector.tensor_tensor(step2[:], unit[:, 1:2], unit[:, 3:4], ALU.mult))
            dve.wait_ge(s("hid_ready"), 2 * FT)
            for half in range(2):
                c = slice(512 * half, 512 * half + 512)
                nc.vector.tensor_scalar(h_lo[:, :, c], hid[:, :, c], inv[:, 3:4], TINY, ALU.mult, ALU.min, saturate=False).then_inc(s("hq_ready"), 1)
                nc.vector.tensor_scalar(h_hi[:, :, c], hid[:, :, c], half_inv[:], TINY / 2, ALU.mult, ALU.max, saturate=False).then_inc(s("hq_ready"), 1)
            dve.wait_ge(s("bias_ps"), 1)
            link(nc.vector.scalar_tensor_tensor(out=xb[:], in0=ps_a[:, 0, 0:E].unsqueeze(1).to_broadcast([P, NPAIR, E]), scalar=step2[:, 0:1],
                                                in1=x2[:], op0=ALU.mult, op1=ALU.add))
            for n in range(NPAIR):
                dve.wait_ge(s("fc2_ready"), n + 1)
                nc.vector.scalar_tensor_tensor(out=res[:, n, :], in0=ps_t[:, n % 4, 0:E], scalar=step2[:, 0:1], in1=xb[:, n, :],
                                               op0=ALU.mult, op1=ALU.add).then_inc(s("res_ready"), 1)


def constants():
    import numpy as np
    f = np.float32
    c = np.zeros((P, C_END), f)
    j = np.arange(D // 2, dtype=f)
    theta = f(10000.0) ** (f(-2.0) * j / f(D))
    ang = (np.arange(T, dtype=f) + f(1.0))[:, None] * theta[None, :].astype(f)
    ang = np.concatenate([ang, ang], -1)
    c[:, C_COS:C_COS + D] = np.tile(np.cos(ang), (2, 1))
    sin = np.sin(ang)
    sin[:, :D // 2] *= -1
    c[:, C_SIN:C_SIN + D] = np.tile(sin, (2, 1))
    for h in range(H):
        c[D * h:D * h + D, C_HEAD + h] = 1.0
    c[:, C_ID:C_ID + P] = np.eye(P, dtype=f)
    for b in range(2):
        for h in range(H):
            for d in range(D):
                row, col = 32 * (h % 4) + 16 * b + d, P * (h // 4) + 64 * b + D * h + d
                c[row, C_NUM + col] = 1.0
                c[row + D, C_DEN + col] = 1.0
    for h in range(H):
        for d in range(D):
            row = 32 * (h % 4) + 16 * (h // 4) + d
            c[row, C_NUM2 + D * h + d] = 1.0
            c[row + D, C_DEN2 + D * h + d] = 1.0
    c[64:, C_STEP:C_STEP + T] = np.eye(T, dtype=f)
    t = np.arange(T)
    c[64:, C_MASK:C_MASK + T] = np.where(t[None, :] > t[:, None], f(-1e30), f(0))
    one = 0x3F80
    cb = np.zeros((P, P + 16 * T), np.uint16)
    cb[:, :P] = one * np.eye(P, dtype=np.uint16)
    for part in range(2):
        for j2 in range(16):
            cb[16 * part + j2, P + T * j2:P + T * j2 + T] = one
    return c, cb


def kernel(x, ctx_2048, L0_attn_Wq, L0_attn_bq, L0_attn_Wk, L0_attn_bk, L0_attn_Wv, L0_attn_bv, L0_attn_Wo,
           L0_attn_bo, L0_xattn_gamma, L0_ffn_w_fc, L0_ffn_w_proj):
    import numpy as np
    import concourse.bacc as bacc
    from concourse.bass_utils import run_bass_kernel_spmd
    x, ctx, wq, bq, wk, bk, wv, bv, wo, bo, gamma, wfc, wproj = (np.asarray(a) for a in (
        x, ctx_2048, L0_attn_Wq, L0_attn_bq, L0_attn_Wk, L0_attn_bk, L0_attn_Wv, L0_attn_bv, L0_attn_Wo, L0_attn_bo,
        L0_xattn_gamma, L0_ffn_w_fc, L0_ffn_w_proj))
    wq = wq.reshape(H, G, D, E).transpose(1, 0, 2, 3).reshape(E, E)
    bq = bq.reshape(H, G, D).transpose(1, 0, 2).reshape(E)
    cf, cb = constants()
    arrays = {
        "x": x.reshape(B * T, E),
        "ctxt": ctx.reshape(B * T, E),
        "ctxt_t": ctx.reshape(B * T, E).T,
        "wqkv": np.concatenate([wq, wk, wv]).T,
        "bqkv": np.concatenate([bq, bk, bv])[None],
        "wo": wo.reshape(E, H, G, D).transpose(1, 3, 2, 0).reshape(H * D, G, E),
        "bo": bo,
        "gamma": gamma.reshape(1),
        "wfc": wfc.T,
        "wproj": wproj.T,
        "cf": cf,
        "cb": cb,
    }
    nc = bacc.Bacc("TRN2", target_bir_lowering=False, num_devices=1)
    ins, args = {}, {}
    for name, a in arrays.items():
        a = np.ascontiguousarray(a)
        ins[f"in_{name}"] = a
        args[name] = nc.dram_tensor(f"in_{name}", a.shape, mybir.dt.from_np(a.dtype), kind="ExternalInput").ap()
    out = nc.dram_tensor("out_x", (B * T, E), F32, kind="ExternalOutput").ap()
    build(nc, **args, out=out)
    r = run_bass_kernel_spmd(nc, [ins], core_ids=[0])
    return r.results[0]["out_x"].reshape(B, T, E)
```

```python
from contextlib import ExitStack

import concourse.bass as bass
from concourse import mybir

ALU = mybir.AluOpType
ACT = mybir.ActivationFunctionType
AX = mybir.AxisListType
F32 = mybir.dt.float32
BF16 = mybir.dt.bfloat16
FP8 = mybir.dt.float8e4
U32 = mybir.dt.uint32
U16 = mybir.dt.uint16

P = 128
EPS = 1e-5
B, T, E = 16, 64, 256
H, G, D = 8, 4, 8
NPAIR = B // 2
SCALE = float(D) ** -0.5
F = 4 * E
KT, FT = E // P, F // P
QKV = E + 2 * H * D
FP8_MAX = 448.0
H_CHUNKS = ((0, 1), (1, 2), (2, 4), (4, 6), (6, NPAIR))
TINY = 2.0 ** -5

C_COS, C_SIN, C_ID, C_NUM, C_DEN, C_NUM2, C_DEN2, C_END = 0, 8, 16, 144, 400, 656, 720, 784
B_ID, B_HEAD, B_TOKEN, B_MASK, B_NMAX, B_END = 0, P, P + 16 * T, 2 * P + 16 * T, 2 * P + 24 * T, 6 * P + 24 * T
PARTS_Q = (0, 1, 2, 0, 1, 0)
PARTS_K = (0, 0, 0, 1, 1, 2)
SPLIT = len(PARTS_Q) * D
PAIR_ROWS = 2 * SPLIT
ROWS = PAIR_ROWS + 4


def build(nc, x, ctxt, ctxt_t, wqkv, bqkv, wo, bo, gamma, wfc, wproj, cf, cb, ck, out):
    with ExitStack() as stack:
        def sb(name, shape, dt=F32):
            return stack.enter_context(nc.sbuf_tensor(name, shape, dt))

        def sem(name):
            return stack.enter_context(nc.semaphore(name))

        bank = [stack.enter_context(nc.psum_tensor(f"bank{i}", [P, 512], F32)) for i in range(2)]
        ps_a = stack.enter_context(nc.psum_tensor("ps_a", [P, 2, 512], F32))
        ps_t = stack.enter_context(nc.psum_tensor("ps_t", [P, 4, 512], F32))

        x_in = sb("x_in", [P, NPAIR, E])
        xb = sb("xb", [P, NPAIR, E])
        x1 = sb("x1", [P, NPAIR, E])
        x2 = sb("x2", [P, NPAIR, E])
        ctx_t = sb("ctx_t", [P, 2, B, T])
        const = sb("const", [P, C_END])
        constb = sb("constb", [P, B_NMAX], BF16)
        w_qkv = sb("w_qkv", [P, KT, QKV])
        b_qkv = sb("b_qkv", [1, QKV])
        b_rest = sb("b_rest", [1, QKV])
        b_parts = sb("b_parts", [1, 3, QKV], BF16)
        b_rows = sb("b_rows", [3, QKV], BF16)
        ones = sb("ones", [3, P], BF16)
        w_o = sb("w_o", [P, 2, E])
        bo_bc = sb("bo_bc", [P, E])
        gam = sb("gam", [P, 1])
        neg_half = sb("neg_half", [P, 1])

        wf = sb("wf", [P, KT, F])
        wp = sb("wp", [P, FT, E])

        stats = sb("stats", [P, NPAIR, 6])
        mv = sb("mv", [P, NPAIR, 2])
        var = sb("var", [P, NPAIR])
        rstd = sb("rstd", [P, NPAIR])
        xn = sb("xn", [P, 2, E])
        xn_t = sb("xn_t", [P, 2, KT, P])
        rope_c = sb("rope_c", [P, QKV - H * D])
        rope_s = sb("rope_s", [P, QKV - H * D])
        qk = sb("qk", [P, 2, QKV - H * D])
        rest_qk = sb("rest_qk", [P, QKV - H * D])
        NH = QKV // D - H
        split_qk = sb("split_qk", [P, NH, 64], BF16)
        q_t = sb("q_t", [P, 2, 4, 2, G, T], BF16)
        k_z = sb("k_z", [P, 2, 2, 4, P], BF16)
        hid_all = sb("hid_all", [P, FT * B * T])
        hid = hid_all[:].rearrange("p (f t) -> p f t", f=FT)
        QUARTER = FT * B * T // 4
        quarter = [hid_all[:, QUARTER * k:QUARTER * k + QUARTER] for k in range(2)]
        v_z = sb("v_z", [P, 2, H, 32])
        nmax = sb("nmax", [P, 2, 2, H, 2])
        nmax_p = sb("nmax_p", [P, 2, 2, 2, 16], BF16)
        nmax_t = sb("nmax_t", [P, 2, 2, P], BF16)
        probs = quarter[1].rearrange("p (s c q) -> p s c q", s=2, c=4)
        u_sb = sb("u_sb", [P, 2, 2, E])
        rden = sb("rden", [P, E])
        y_t = sb("y_t", [P, 2, E])
        stats2 = sb("stats2", [P, 6])
        mv2 = sb("mv2", [P, 2])
        var2 = sb("var2", [P, 1])
        rstd2 = sb("rstd2", [P, 1])
        x1n = sb("x1n", [P, 2, E])
        rest = sb("rest", [P, 2, E])
        q_parts = sb("q_parts", [P, 2, 3, E], BF16)
        ctx_in = sb("ctx_in", [P, NPAIR, E])
        ctx_rest = sb("ctx_rest", [P, E])
        k_parts = sb("k_parts", [P, 2, 3, E], BF16)
        d_q = nc.dram_tensor("d_q", [B * 4, 2, len(PARTS_Q), D, E], BF16, kind="Internal").ap()
        d_k = nc.dram_tensor("d_k", [B * 4, 2, len(PARTS_K), D, E], BF16, kind="Internal").ap()
        q_st = quarter[0].bitcast(BF16).rearrange("p (r a e) -> p r a e", r=4, a=4)
        k_flat = hid_all[:, 2 * QUARTER:4 * QUARTER]
        k_st = k_flat.bitcast(BF16).rearrange("p (r h a e) -> p r h a e", r=4, h=2, a=4)
        v2_z = sb("v2_z", [P, 2, 2, H, 32])
        nmax2 = sb("nmax2", [P, 2, 2, 2, 4])
        nmax2_p = sb("nmax2_p", [P, 2, 2, 2, 2, 4], BF16)
        nmax2_t = sb("nmax2_t", [16, 2, 2, P], BF16)
        probs2_all = sb("probs2", [P, 4 * 2 * 2 * E])
        probs2 = probs2_all[:].rearrange("p (r h l q) -> p r h l q", r=4, h=2, l=2)
        u2_sb = u_sb[:, 0]
        rden2 = rden
        y2 = sb("y2", [P, E])
        stats3 = sb("stats3", [P, 6])
        mv3 = sb("mv3", [P, 2])
        var3 = sb("var3", [P, 1])
        rstd3 = sb("rstd3", [P, 1])
        top_x = sb("top_x", [P, NPAIR])
        top = sb("top", [P, 4])
        top_all = sb("top_all", [P, 4])
        unit = sb("unit", [P, 4])
        inv = sb("inv", [P, 4])
        half_inv = sb("half_inv", [P, 1])
        step1 = sb("step1", [P, 1])
        step2 = sb("step2", [P, 1])
        magic = sb("magic", [P, NPAIR * E])
        wf8 = sb("wf8", [P, KT, F], BF16)
        wp8 = sb("wp8", [P, 2, FT, E], BF16)
        x8 = ctx_in[:, 0:4].bitcast(BF16).rearrange("p n (a d) -> p (n a) d", a=2)
        x8_t = ctx_in[:, 4:8].bitcast(BF16).rearrange("p (k m) d -> p k (m d)", k=KT)
        minus_tiny = sb("minus_tiny", [P, P], BF16)
        tops = sb("tops", [P, 2 * FT])
        h_lo, h_hi = (probs2_all[:, 2048 * k:2048 * k + 2048].bitcast(FP8).rearrange("p (f t) -> p f t", f=FT) for k in range(2))
        res = x1

        names = """
        ld_bias ld_x ld_xr ld_const ld_w ld_small ld_nmax ld_wo ld_ffn ld_ctx
        setup_pool setup_dve bias_parts b_ready kst_zero kst_ones passed
        var_ready rstd_ready xn_ready xt_ps xt_ready proj_ready hi_ready qk_ready mid_ready lo_ready copied
        kt_ps kt_ready qt_ps qt_ready v_ready s_ready max_done nmax_ready mt_ps mt_ready t_ready exp_done
        u_ready us_ready nd_ready inverted y_ready w_ready x1_ready var2_ready rstd2_ready x1n_ready
        parts_ready kparts_ready
        s2_ready max2_done nmax2_ready mt2_ps mt2_ready t2_ready exp2_done v2_ready pv2_done us2_ready nd2_ready
        nd2_read x2_ready stat3_ready mv3_ready var3_ready rstd3_ready centred x3_ready
        top_ready top_all_ready inv_ready ws_ready wf8_ready wp8_ready topx_ready xs_ready x8_ready x8t_ps x8t_ready
        fc1_ready relu_ready hid_ready step2_ready bias_ps bias_ready base_ready hq_ready fc2_ready res_ready stored
        chain_a chain_bias chain_rope chain_rest chain_max chain_norm chain_max2 chain_parts chain_context
        chain_round chain_ffn
        """.split()
        sems = {name: sem(name) for name in names}

        def s(name):
            return sems[name]

        q_written = [sem(f"q_written{u}") for u in range(2)]
        k_written = [sem(f"k_written{u}") for u in range(2)]
        qk_loaded = [sem(f"qk_loaded{r}") for r in range(4)]
        m_loaded = [sem(f"m_loaded{r}") for r in range(4)]
        block = stack.enter_context(nc.Block())

        def wait(eng, name, value, alone=False):
            if not isinstance(value, int) or value > 0:
                eng.wait_ge(s(name) if isinstance(name, str) else name, value)
                if alone and not isinstance(value, int):
                    eng.sem_inc(s("passed"), 1)

        def steps(eng, body):
            for n in range(2):
                body(n, n)
            with eng.Fori(2, NPAIR - 3, 2) as i:
                for v in range(2):
                    body(i + v, v)
            for n in range(NPAIR - 2, NPAIR + 1):
                body(n, n % 2)

        def has(n):
            return not isinstance(n, int) or 0 <= n < NPAIR

        def steps2(eng, body):
            body(0, 0)
            with eng.Fori(1, B - 6, 4) as i:
                for v in range(4):
                    body(i + v, (1 + v) % 4)
            for n in range(B - 3, B):
                body(n, n % 4)

        def loads_of(n, r, each):
            return each // 4 * (n - r) + each

        def chained(eng, name, n, per_pair):
            done = [0]

            def link(ins, alone=False):
                done[0] += 1
                assert done[0] <= per_pair
                ins.then_inc(s(name), 1)
                wait(eng, name, n * per_pair + done[0], alone)
            return link

        def tok(ap):
            return ap.rearrange("(n p) d -> p n d", p=P)

        def at(ap, n):
            return ap[:, n, :] if isinstance(n, int) else ap[:, bass.ds(n, 1), :]

        def out_ps(n):
            return ps_t[:, 3, 0:E] if isinstance(n, int) and n == NPAIR - 1 else bank[0][:, 0:E]

        def x8_ps(half, k):
            return bank[half][:, 256 * k:256 * k + 256].bitcast(BF16)

        fc2_ps = [ps_t[:, i, 0:E] for i in range(4)] + [bank[0][:, 0:E], bank[1][:, 0:E], ps_a[:, 1, 0:E], ps_t[:, 0, 0:E]]

        @block.sync
        def _(sp):
            sp.dma_start(b_qkv[:], bqkv).then_inc(s("ld_bias"), 16)
            sp.dma_start(x_in[:, 0:2], tok(x)[:, 0:2]).then_inc(s("ld_x"), 16)
            sp.dma_start(const[:], cf).then_inc(s("ld_const"), 16)
            sp.dma_start(w_qkv[:], wqkv.rearrange("(k p) n -> p k n", p=P)).then_inc(s("ld_w"), 16)
            sp.wait_ge(s("bias_parts"), 1)
            for part in range(3):
                sp.dma_start(b_rows[part:part + 1], b_parts[:, part]).then_inc(s("b_ready"), 16)
            sp.dma_start(constb[:].bitcast(U16), cb[:, 0:B_NMAX]).then_inc(s("ld_small"), 16)
            sp.dma_start(nmax_t[:].rearrange("p u g q -> p (u g q)").bitcast(U16), cb[:, B_NMAX:B_END]).then_inc(s("ld_nmax"), 16)
            sp.dma_start(x_in[:, 2:NPAIR], tok(x)[:, 2:NPAIR]).then_inc(s("ld_xr"), 16)
            sp.dma_start(bo_bc[:], bo.partition_broadcast(P)).then_inc(s("ld_wo"), 16)
            sp.dma_start(gam[:], gamma.partition_broadcast(P)).then_inc(s("ld_wo"), 16)
            sp.dma_start(w_o[:], wo).then_inc(s("ld_wo"), 16)
            sp.dma_start(wf[:], wfc.rearrange("(k p) n -> p k n", p=P)).then_inc(s("ld_ffn"), 16)
            sp.dma_start(wp[:], wproj.rearrange("(k p) n -> p k n", p=P)).then_inc(s("ld_ffn"), 16)
            sp.dma_start(ctx_in[:], tok(ctxt)).then_inc(s("ld_ctx"), 16)
            sp.dma_start(ctx_t[:], ctxt_t.rearrange("(l p) (b t) -> p l b t", p=P, t=T)).then_inc(s("ld_ctx"), 16)

            def spread(d_st, parts, src, n, written):
                rows = d_st.rearrange("(n a) h c d e -> n c (a h) d e", a=8)
                for c, part in enumerate(parts):
                    dst = rows[n, c] if isinstance(n, int) else rows[bass.ds(n, 1), c].rearrange("n a d e -> (n a) d e")
                    sp.dma_start(dst, src[:, part, :]).then_inc(written, 16)

            def load(n, r):
                q_src, k_src = (d_st[4 * n:4 * n + 4] if isinstance(n, int) else d_st[bass.ds(4 * n, 4)] for d_st in (d_q, d_k))
                sp.dma_start(q_st[0:PAIR_ROWS, r], q_src.rearrange("a h c d e -> (h c d) a e")).then_inc(qk_loaded[r], 16)
                for hp in range(2):
                    sp.dma_start(k_st[SPLIT * hp:SPLIT * hp + SPLIT, r, hp], k_src[:, hp].rearrange("a c d e -> (c d) a e")
                                 ).then_inc(qk_loaded[r], 16)

            def maxima(n, r):
                wait(sp, "mt2_ready", n + 1)
                sp.dma_start(q_st[PAIR_ROWS:ROWS, r], nmax2_t[:, r % 2].rearrange("p g q -> p (g q)")
                             ).then_inc(m_loaded[r], 16)

            def body(n, u):
                if isinstance(n, int) and n == NPAIR:
                    maxima(0, 0)
                if isinstance(n, int) and n == NPAIR - 1:
                    sp.wait_ge(s("kst_zero"), 1)
                    sp.dma_start(k_st[PAIR_ROWS:ROWS].rearrange("p r h a e -> p (r h a e)").bitcast(U16), ck).then_inc(s("kst_ones"), 16)
                    for v in range(2):
                        sp.wait_ge(q_written[v], 16 * 6 + 1)
                        sp.wait_ge(k_written[v], 16 * 6)
                    for m in range(3):
                        load(m, m)
                if has(n):
                    wait(sp, "kparts_ready", n + 1)
                    spread(d_k, PARTS_K, k_parts[:, u], n, k_written[u])
                if has(n - 2):
                    wait(sp, "parts_ready", n - 1)
                    spread(d_q, PARTS_Q, q_parts[:, u], n - 2, q_written[u])
                if isinstance(n, int) and n == NPAIR:
                    wait(sp, "parts_ready", n)
                    spread(d_q, PARTS_Q, q_parts[:, 1 - u], n - 1, q_written[1 - u])
            steps(sp, body)

            def body2(n, r):
                if not isinstance(n, int) or n + 1 < B:
                    maxima(n + 1, (r + 1) % 4)
                if not isinstance(n, int) or n + 3 < B:
                    wait(sp, "t2_ready", 4 * n)
                    load(n + 3, (r + 3) % 4)
                if isinstance(n, int) and n == 0:
                    for u in range(2):
                        sp.wait_ge(q_written[u], 16 * 6 * 4 + 1)
                        sp.wait_ge(k_written[u], 16 * 6 * 4)
            steps2(sp, body2)
            for n in range(NPAIR):
                sp.wait_ge(s("res_ready"), n + 1)
                sp.dma_start(tok(out)[:, n, :], res[:, n, :]).then_inc(s("stored"), 16)
            sp.wait_ge(s("stored"), 16 * NPAIR)

        @block.gpsimd
        def _(pool):
            nc.gpsimd.memset(ones[:], 1.0).then_inc(s("setup_pool"), 1)
            nc.gpsimd.memset(neg_half[:], -0.5).then_inc(s("setup_pool"), 1)
            for u in range(2):
                nc.gpsimd.memset(v_z[:, u], 0.0).then_inc(s("setup_pool"), 1)
            pool.wait_ge(s("setup_pool"), 4)
            for u in range(2):
                nc.gpsimd.memset(v_z[0:64, u, :, 8:16], 1.0).then_inc(s("setup_pool"), 1)
            for u in range(2):
                pool.wait_ge(s("setup_pool"), 6 + u)
                nc.gpsimd.memset(v_z[64:128, u, :, 24:32], 1.0).then_inc(s("setup_pool"), 1)
            pool.wait_ge(s("setup_pool"), 8)

            def rstd_a(first, end, turn):
                pool.wait_ge(s("var_ready"), turn)
                nc.gpsimd.tensor_tensor(rstd[:, first:end], var[:, first:end], neg_half[:].to_broadcast([P, end - first]), ALU.pow
                                        ).then_inc(s("rstd_ready"), 1)

            def rstd_c(n):
                wait(pool, "var2_ready", n + 1)
                nc.gpsimd.tensor_tensor(rstd2[:], var2[:], neg_half[:], ALU.pow).then_inc(s("rstd2_ready"), 1)

            def parts_c(n, u):
                link = chained(pool, "chain_parts", n, 3)
                wait(pool, "x1n_ready", n + 1)
                wait(pool, q_written[u], 48 * (n - u) + 1, alone=True)
                link(nc.gpsimd.tensor_copy(q_parts[:, u, 0, :], x1n[:, u, :]))
                link(nc.gpsimd.tensor_tensor(rest[:, u, :], x1n[:, u, :], q_parts[:, u, 0, :], ALU.subtract), alone=True)
                link(nc.gpsimd.tensor_copy(q_parts[:, u, 1, :], rest[:, u, :]))
                nc.gpsimd.tensor_tensor(q_parts[:, u, 2, :], rest[:, u, :], q_parts[:, u, 1, :], ALU.subtract).then_inc(s("parts_ready"), 1)

            def context(n, u):
                link = chained(pool, "chain_context", n, 3)
                wait(pool, k_written[u], 48 * (n - u), alone=True)
                c_n = at(ctx_in, n)
                k0, k1, k2 = (k_parts[:, u, c, :] if isinstance(n, int) else k_parts[:, u, c:c + 1, :] for c in range(3))
                r_n = ctx_rest[:] if isinstance(n, int) else ctx_rest[:].unsqueeze(1)
                link(nc.gpsimd.tensor_copy(k0, c_n), alone=True)
                link(nc.gpsimd.tensor_tensor(r_n, c_n, k0, ALU.subtract), alone=True)
                link(nc.gpsimd.tensor_copy(k1, r_n), alone=True)
                nc.gpsimd.tensor_tensor(k2, r_n, k1, ALU.subtract).then_inc(s("kparts_ready"), 1)

            def reduce_top(k):
                pool.wait_ge(s("top_ready"), k + 1)
                nc.gpsimd.partition_all_reduce(top_all[:, k:k + 1], top[:, k:k + 1], P, bass.bass_isa.ReduceOp.max
                                               ).then_inc(s("top_all_ready"), 1)

            def body(n, u):
                if isinstance(n, int) and n == 0:
                    for k in range(2):
                        reduce_top(k)
                if has(n - 2):
                    rstd_c(n - 2)
                    parts_c(n - 2, u)
                if isinstance(n, int) and n == NPAIR:
                    rstd_c(n - 1)
                    parts_c(n - 1, 1 - u)
                if has(n):
                    context(n, u)
                if isinstance(n, int) and n == NPAIR - 2:
                    nc.gpsimd.memset(k_flat, 0.0).then_inc(s("kst_zero"), 1)

            for u in range(2):
                pool.sem_inc(q_written[u], 1)
            pool.sem_inc(s("x3_ready"), 1)
            rstd_a(0, 2, 1)
            rstd_a(2, NPAIR, 2)
            pool.wait_ge(s("ld_wo"), 48)
            pool.wait_ge(s("ld_x"), 16)
            pool.wait_ge(s("ld_xr"), 16)
            nc.gpsimd.tensor_tensor(xb[:], x_in[:], bo_bc[:].unsqueeze(1).to_broadcast([P, NPAIR, E]), ALU.add).then_inc(s("setup_pool"), 1)
            nc.gpsimd.memset(v2_z[:], 0.0).then_inc(s("setup_pool"), 1)
            pool.wait_ge(s("setup_pool"), 10)
            for hh in range(2):
                for u in range(2):
                    nc.gpsimd.memset(v2_z[:, u, :, 4 * hh:4 * hh + 4, 16 * hh + 8:16 * hh + 16], 1.0).then_inc(s("setup_pool"), 1)
            pool.wait_ge(s("ld_ctx"), 32)
            steps(pool, body)

            def values(n, u):
                wait(pool, "pv2_done", 2 * (n - 1))
                for hh in range(2):
                    cols = slice(32 * hh, 32 * hh + 32)
                    src = (ctx_t[:, :, n, cols] if isinstance(n, int)
                           else ctx_t[:, :, bass.ds(n, 1), cols].rearrange("p l n d -> p l (n d)"))
                    ins = nc.gpsimd.tensor_copy(v2_z[:, u, :, 4 * hh:4 * hh + 4, 16 * hh:16 * hh + D], src.rearrange("p l (c d) -> p l c d", d=D))
                ins.then_inc(s("v2_ready"), 1)

            values(0, 0)
            values(1, 1)

            def normalise(n):
                known = isinstance(n, int)
                cols = slice(P * (n - 2), P * n) if known else bass.ds(P * (n - 2), 2 * P)
                wait(pool, "var3_ready", n)
                nc.gpsimd.tensor_tensor(rstd3[:], var3[:], neg_half[:], ALU.pow).then_inc(s("rstd3_ready"), 2)
                wait(pool, "rstd3_ready", n, alone=True)
                src, dst = (a[:].rearrange("p n d -> p (n d)")[:, cols] for a in (x2, xb))
                nc.gpsimd.tensor_tensor(dst, src, mv3[:, 0:1].to_broadcast([P, 2 * P]), ALU.subtract).then_inc(s("centred"), 2)
                wait(pool, "centred", n, alone=True)
                nc.gpsimd.tensor_tensor(dst, dst, rstd3[:].to_broadcast([P, 2 * P]), ALU.mult).then_inc(s("x3_ready"), 2)

            def body2(n, r):
                if not isinstance(n, int) or n + 2 < B:
                    values(n + 2, r % 2)
                if r % 2 == 0 and (not isinstance(n, int) or n > 0):
                    normalise(n)
            steps2(pool, body2)
            normalise(B)

            nc.gpsimd.memset(minus_tiny[:], -TINY).then_inc(s("setup_pool"), 1)
            reduce_top(2)
            pool.wait_ge(s("wp8_ready"), 1)
            nc.gpsimd.tensor_tensor(wp8[:, 1], wp8[:, 0], wp8[:, 0], ALU.add).then_inc(s("wp8_ready"), 1)
            reduce_top(3)
            pool.wait_ge(s("bias_ready"), 1)
            nc.gpsimd.tensor_tensor(xb[:], x2[:], y2[:].unsqueeze(1).to_broadcast([P, NPAIR, E]), ALU.add).then_inc(s("base_ready"), 1)

        @block.tensor
        def _(pe):
            ident = const[:, C_ID:C_ID + P]
            pe.wait_ge(s("ld_const"), 16)

            def turn_x(n, u):
                wait(pe, "xn_ready", n + 1)
                wait(pe, "kt_ready", n - 1)
                wait(pe, "x1_ready", n - 3)
                for k in range(KT):
                    mm = nc.tensor.transpose(bank[0][:, P * k:P * k + P], xn[:, u, P * k:P * k + P], ident)
                mm.then_inc(s("xt_ps"), 1)

            def project(n, u):
                wait(pe, "xt_ready", n + 1)
                wait(pe, "v_ready", n)
                nc.tensor.matmul(bank[1][:, 0:QKV], ones[:], b_rows[:], start=True, stop=False)
                for k in range(KT):
                    mm = nc.tensor.matmul(bank[1][:, 0:QKV], xn_t[:, u, k, :], w_qkv[:, k, :], start=False, stop=(k == KT - 1))
                mm.then_inc(s("proj_ready"), 1)

            def turn_k(n, u):
                wait(pe, "lo_ready", n + 1)
                wait(pe, "copied", n + 1, alone=True)
                for ht in range(4):
                    mm = nc.tensor.transpose(bank[0][:, E:2 * E].bitcast(BF16)[:, P * ht:P * ht + P],
                                             split_qk[:, G * H + 2 * ht:G * H + 2 * ht + 2, :].rearrange("p h c -> p (h c)"), constb[:, 0:P])
                mm.then_inc(s("kt_ps"), 1)

            def turn_q(n, u, half):
                wait(pe, "qt_ready", 2 * n + half)
                for g in range(2):
                    for ht in range(4):
                        head = H * (2 * half + g) + 2 * ht
                        mm = nc.tensor.transpose(ps_a[:, 0, :].bitcast(BF16)[:, P * (4 * g + ht):P * (4 * g + ht) + P],
                                                 split_qk[:, head:head + 2, :].rearrange("p h c -> p (h c)"), constb[:, 0:P])
                mm.then_inc(s("qt_ps"), 1)

            def scores_q(n, u, k):
                b, gp = k // 2, k % 2
                if k == 0:
                    wait(pe, "qt_ready", 2 * n + 2)
                    wait(pe, "kt_ready", n + 1)
                    wait(pe, "exp_done", 2 * n)
                if k >= 2:
                    wait(pe, "max_done", 4 * n + k - 1)
                nc.tensor.matmul(ps_t[:, 2 + k % 2, :], constb[:, B_TOKEN:B_TOKEN + P], constb[:, B_MASK:B_MASK + H * T],
                                 start=True, stop=False)
                for ht in range(4):
                    mm = nc.tensor.matmul(ps_t[:, 2 + k % 2, P * ht:P * ht + P], q_t[:, u, ht, b, 2 * gp:2 * gp + 2, :].rearrange("p g t -> p (g t)"),
                                          k_z[:, u, :, ht, T * b:T * b + T], start=False, stop=(ht == 3))
                mm.then_inc(s("s_ready"), 1)

            def turn_nmax(n, u):
                wait(pe, "nmax_ready", n + 1)
                pst = ps_t[0:32, 2, 0:P].bitcast(BF16)
                for gp in range(2):
                    mm = nc.tensor.transpose(pst[:, P * gp:P * gp + P], nmax_p[:, u, gp].rearrange("p a b -> p (a b)"), constb[:, 0:P])
                mm.then_inc(s("mt_ps"), 1)

            def scores_k(n, u, hh):
                if hh == 0:
                    wait(pe, "mt_ready", n + 1)
                wait(pe, "exp_done", 2 * n - 1 if hh == 0 else 0)
                for c in range(4):
                    for b in range(2):
                        h = 4 * hh + c
                        o = ps_t[64 * b:64 * b + 64, 2 * hh + c // 2, E * (c % 2):E * (c % 2) + E]
                        nc.tensor.matmul(o, k_z[:, u, h % 2, h // 2, T * b:T * b + T], q_t[:, u, h // 2, b].rearrange("p g t -> p (g t)"),
                                         start=True, stop=False)
                        j = 2 * h + b
                        mm = nc.tensor.matmul(o, constb[:, B_HEAD + T * j:B_HEAD + T * j + T],
                                              nmax_t[:, u].rearrange("p g q -> p (g q)"), start=False, stop=True)
                mm.then_inc(s("t_ready"), 1)

            def weigh_v(n, u, hh):
                if hh == 0:
                    wait(pe, "v_ready", n + 1)
                wait(pe, "exp_done", 2 * n + hh + 1)
                for c in range(4):
                    mm = nc.tensor.matmul(ps_a[32 * c:32 * c + 32, 1, E * hh:E * hh + E], v_z[:, u, 4 * hh + c, :],
                                          probs[:, hh, c, :], start=True, stop=True)
                if hh == 1:
                    mm.then_inc(s("u_ready"), 1)

            def sort_heads(n, u):
                wait(pe, "us_ready", n + 1)
                for k, col in enumerate((C_DEN, C_NUM)):
                    for b in range(2):
                        for hh in range(2):
                            for gi in range(2):
                                o = ps_a[64 * gi:64 * gi + 64, 1, E * k:E * k + E].rearrange("p (g b t) -> p g b t", b=2, t=T)[:, :, b]
                                src = u_sb[:, u, hh, :].rearrange("p (g i t) -> p g i t", i=2, t=T)[:, :, gi]
                                c0 = col + P * hh + 64 * b
                                mm = nc.tensor.matmul(o, const[:, c0:c0 + 64], src, start=(hh == 0), stop=(hh == 1), skip_group_check=True)
                mm.then_inc(s("nd_ready"), 1)

            def project_out(n, u):
                wait(pe, "y_ready", n + 1, alone=True)
                if has(n + 2):
                    wait(pe, "kt_ready", n + 3)
                for gg in range(2):
                    mm = nc.tensor.matmul(out_ps(n), y_t[:, u, P * gg:P * gg + P], w_o[:, gg, :], start=(gg == 0), stop=(gg == 1))
                mm.then_inc(s("w_ready"), 1)

            def scores(n, r, ht, which=(0, 1)):
                for hp in which:
                    if ht == 0 and hp == 0:
                        wait(pe, qk_loaded[r], loads_of(n, r, 48))
                    wait(pe, "max2_done", 8 * n + 2 * ht + hp - 1)
                    for half in range(2):
                        mm = nc.tensor.matmul(bank[hp][:, E * half:E * half + E], q_st[0:PAIR_ROWS, r, ht, P * half:P * half + P],
                                              k_st[0:PAIR_ROWS, r, hp, ht, :], start=True, stop=True)
                    mm.then_inc(s("s2_ready"), 1)

            def turn_maxima(n, r):
                wait(pe, "nmax2_ready", n + 1)
                wait(pe, "nd2_read", n - 1 - r % 2)
                dst = ps_a[0:16, 1, 0:P].bitcast(BF16)
                for half in range(2):
                    mm = nc.tensor.transpose(dst[:, P * half:P * half + P],
                                             nmax2_p[:, r % 2, half].rearrange("p h c t -> p (h c t)"), constb[:, 0:P])
                mm.then_inc(s("mt2_ps"), 1)

            def scores_t(n, r, ht):
                if ht == 1 and isinstance(n, int):
                    pe.wait_ge(s("x1_ready"), NPAIR)
                if ht == 0:
                    wait(pe, m_loaded[r], loads_of(n, r, 16))
                    if isinstance(n, int) and n == 0:
                        pe.wait_ge(s("kst_ones"), 16)
                wait(pe, "exp2_done", 4 * n + ht - 1)
                for hp in range(2):
                    for half in range(2):
                        mm = nc.tensor.matmul(ps_t[:, 2 * (ht % 2) + hp, E * half:E * half + E],
                                              k_st[0:ROWS, r, hp, ht, P * half:P * half + P], q_st[0:ROWS, r, ht, :], start=True, stop=True)
                mm.then_inc(s("t2_ready"), 1)

            def weigh(n, r, hh, half):
                b = r % 2
                wait(pe, "exp2_done", 4 * n + 2 * hh + 2)
                if hh == 0 and half == 0:
                    wait(pe, "v2_ready", n + 1)
                    if b == 0:
                        wait(pe, "us2_ready", n)
                for c in range(4):
                    mm = nc.tensor.matmul(ps_a[32 * c:32 * c + 32, 0, E * b:E * b + E], v2_z[:, b, half, 4 * hh + c, :],
                                          probs2[:, 2 * hh + c // 2, c % 2, half, :],
                                          start=(b == 0 and hh == 0 and half == 0), stop=(hh == 1 and half == 1),
                                          skip_group_check=True)
                if half == 1:
                    mm.then_inc(s("pv2_done"), 1)

            def gather_heads(n):
                wait(pe, "us2_ready", n)
                wait(pe, "mt2_ready", n + 2 if not isinstance(n, int) else min(n + 2, B))
                wait(pe, "nd2_read", n - 1)
                for k, col in enumerate((C_NUM2, C_DEN2)):
                    for b in range(2):
                        mm = nc.tensor.matmul(ps_a[64 * b:64 * b + 64, 1, E * k:E * k + E], const[:, col:col + 64],
                                              u2_sb[:, b, :], start=True, stop=True)
                    mm.then_inc(s("nd2_ready"), 1)

            turn_x(0, 0)
            pe.wait_ge(s("ld_w"), 16)
            pe.wait_ge(s("b_ready"), 48)
            pe.wait_ge(s("setup_pool"), 1)
            project(0, 0)
            pe.wait_ge(s("ld_small"), 16)
            turn_k(0, 0)
            turn_q(0, 0, 0)
            turn_q(0, 0, 1)
            turn_x(1, 1)
            project(1, 1)
            pe.wait_ge(s("setup_pool"), 8)
            pe.wait_ge(s("ld_nmax"), 16)
            pe.wait_ge(s("ld_wo"), 48)

            def body(n, u):
                last = isinstance(n, int) and n == NPAIR
                if has(n):
                    scores_q(n, u, 0)
                    scores_q(n, u, 1)
                if has(n + 2):
                    turn_x(n + 2, u)
                if has(n - 1):
                    weigh_v(n - 1, 1 - u, 1)
                if last:
                    pe.wait_ge(s("x1_ready"), NPAIR - 1)
                    scores(0, 0, 0)
                    scores(0, 0, 1)
                if has(n):
                    scores_q(n, u, 2)
                    scores_q(n, u, 3)
                if has(n - 1):
                    sort_heads(n - 1, 1 - u)
                if last:
                    scores(0, 0, 2)
                    scores(0, 0, 3)
                if has(n + 1):
                    turn_k(n + 1, 1 - u)
                    turn_q(n + 1, 1 - u, 0)
                if has(n):
                    turn_nmax(n, u)
                if has(n + 2):
                    project(n + 2, u)
                if has(n):
                    scores_k(n, u, 0)
                if has(n + 1):
                    turn_q(n + 1, 1 - u, 1)
                if has(n):
                    scores_k(n, u, 1)
                if has(n - 1):
                    project_out(n - 1, 1 - u)
                if last:
                    turn_maxima(0, 0)
                if has(n):
                    weigh_v(n, u, 0)
            pe.sem_inc(s("nd2_ready"), 1)
            steps(pe, body)

            for ht in range(4):
                scores(1, 1, ht)

            def body2(n, r):
                known = isinstance(n, int)
                ahead = not known or n + 2 < B
                before = not known or n > 0

                def ahead_scores(ht, hp):
                    if ahead:
                        scores(n + 2, (r + 2) % 4, ht, (hp,))

                ahead_scores(0, 0)
                scores_t(n, r, 0)
                ahead_scores(0, 1)
                if not known or n + 1 < B:
                    turn_maxima(n + 1, (r + 1) % 4)
                if before:
                    weigh(n - 1, (r - 1) % 4, 1, 0)
                ahead_scores(1, 0)
                scores_t(n, r, 1)
                ahead_scores(1, 1)
                if before:
                    weigh(n - 1, (r - 1) % 4, 1, 1)
                ahead_scores(2, 0)
                scores_t(n, r, 2)
                ahead_scores(2, 1)
                if r % 2 == 0 and before:
                    gather_heads(n)
                weigh(n, r, 0, 0)
                ahead_scores(3, 0)
                scores_t(n, r, 3)
                ahead_scores(3, 1)
                weigh(n, r, 0, 1)
            steps2(pe, body2)
            weigh(B - 1, 3, 1, 0)
            weigh(B - 1, 3, 1, 1)
            gather_heads(B)

            pe.wait_ge(s("x2_ready"), 2 * NPAIR)
            pe.wait_ge(s("setup_pool"), 15)
            pe.wait_ge(s("wp8_ready"), 1)
            for f in range(FT):
                mm = nc.tensor.matmul(ps_a[:, 0, 0:E], minus_tiny[:], wp8[:, 0, f, :], start=(f == 0), stop=(f == FT - 1))
            mm.then_inc(s("bias_ps"), 1)
            def turn_x8(half):
                pe.wait_ge(s("x8_ready"), half + 1)
                for n in range(4):
                    for k in range(KT):
                        mm = nc.tensor.transpose(x8_ps(half, k)[:, P * n:P * n + P], x8[:, 4 * half + n, P * k:P * k + P], constb[:, 0:P])
                mm.then_inc(s("x8t_ps"), 1)

            turn_x8(0)
            pe.wait_ge(s("wf8_ready"), 1)
            for i in range(2 * FT):
                half, f = i // FT, i % FT
                if i == 4:
                    turn_x8(1)
                if f == 0:
                    pe.wait_ge(s("x8t_ready"), 2 * half + 2)
                if i >= 4:
                    pe.wait_ge(s("relu_ready"), i - 3)
                for k in range(KT):
                    mm = nc.tensor.matmul(ps_t[:, i % 4, :], wf8[:, k, P * f:P * f + P], x8_t[:, k, 512 * half:512 * half + 512],
                                          start=(k == 0), stop=(k == KT - 1))
                mm.then_inc(s("fc1_ready"), 1)
            pe.wait_ge(s("wp8_ready"), 2)
            for n in range(NPAIR):
                if n == NPAIR - 1:
                    pe.wait_ge(s("res_ready"), 1)
                for part, h8 in enumerate((h_lo, h_hi)):
                    pe.wait_ge(s("hq_ready"), 2 * sum(first <= n for first, _ in H_CHUNKS[1:]) + part + 1)
                    for f in range(FT):
                        mm = nc.tensor.matmul(fc2_ps[n], h8[:, f, P * n:P * n + P], wp8[:, part, f, :],
                                              start=(part == 0 and f == 0), stop=(part == 1 and f == FT - 1))
                mm.then_inc(s("fc2_ready"), 1)

        @block.scalar
        def _(act):
            def scale_weights(k):
                act.wait_ge(s("inv_ready"), k + 1)
                w = (wf, wp)[k][:].rearrange("p k n -> p (k n)")
                nc.scalar.activation(w, w, ACT.Copy, scale=inv[:, k:k + 1]).then_inc(s("ws_ready"), 1)

            def keep_x(n, u):
                wait(act, "xt_ps", n + 1)
                nc.scalar.copy(xn_t[:, u].rearrange("p k t -> p (k t)"), bank[0][:, 0:2 * P]).then_inc(s("xt_ready"), 1)

            def keep_v(n, u):
                wait(act, "qk_ready", n + 1)
                wait(act, "u_ready", n - 1)
                for b in range(2):
                    r = slice(64 * b, 64 * b + 64)
                    ins = nc.scalar.copy(v_z[r, u, :, 16 * b:16 * b + D],
                                         bank[1][r, E + 64:QKV].rearrange("p (h d) -> p h d", d=D))
                ins.then_inc(s("v_ready"), 1)

            def copies(head0, heads, first, count, step):
                end = first + (count - 1) * step + 1
                return split_qk[:, head0:head0 + heads, 0:SPLIT].rearrange("p h (c d) -> p h c d", d=D)[:, :, first:end:step]

            def copy_part(head0, heads, source, first, count, step):
                src = split_qk[:, head0:head0 + heads, D * source:D * source + D]
                if count > 1:
                    return nc.scalar.copy(copies(head0, heads, first, count, step), src.unsqueeze(2).to_broadcast([P, heads, count, D]))
                return nc.scalar.copy(split_qk[:, head0:head0 + heads, D * first:D * first + D], src)

            def high_parts(n):
                wait(act, "hi_ready", n + 1)
                copy_part(0, G * H, 0, 1, 2, 1)
                copy_part(G * H, H, 0, 3, 2, 2)

            def middle_parts(n):
                wait(act, "mid_ready", n + 1)
                copy_part(0, G * H, 4, 3, 1, 1)
                copy_part(G * H, H, 4, 1, 1, 1).then_inc(s("copied"), 1)

            def keep_k(n, u):
                wait(act, "kt_ps", n + 1)
                wait(act, "t_ready", 2 * (n - 1))
                for hp in range(2):
                    r = slice(64 * hp, 64 * hp + 64)
                    ins = nc.scalar.copy(k_z[r, u, hp].rearrange("p a t -> p (a t)"), bank[0][r, E:2 * E].bitcast(BF16))
                ins.then_inc(s("kt_ready"), 1)

            def keep_q(n, u, half):
                wait(act, "qt_ps", 2 * n + half + 1)
                nc.scalar.copy(q_t[:, u, :, :, 2 * half:2 * half + 2].rearrange("p a b g t -> p (a b) g t"),
                               ps_a[:, 0, :].bitcast(BF16).rearrange("p (g x t) -> p x g t", g=2, t=T)).then_inc(s("qt_ready"), 1)

            def keep_nmax(n, u):
                wait(act, "mt_ps", n + 1)
                nc.scalar.copy(nmax_t[0:32, u].rearrange("p g q -> p (g q)"), ps_t[0:32, 2, 0:P].bitcast(BF16)).then_inc(s("mt_ready"), 1)

            def exp(n, hh):
                wait(act, "t_ready", 2 * n + hh + 1)
                nc.scalar.activation(probs[:, hh].rearrange("p c q -> p (c q)"),
                                     ps_t[:, 2 * hh:2 * hh + 2, :].rearrange("p a b -> p (a b)"), ACT.Exp, scale=SCALE).then_inc(s("exp_done"), 1)

            def keep_sums_a(n, u):
                wait(act, "u_ready", n + 1)
                nc.scalar.copy(u_sb[:, u].rearrange("p b q -> p (b q)"), ps_a[:, 1, :]).then_inc(s("us_ready"), 1)

            keep_x(0, 0)
            act.wait_ge(s("setup_pool"), 8)
            keep_v(0, 0)
            high_parts(0)
            middle_parts(0)
            act.wait_ge(s("setup_dve"), 2)
            keep_k(0, 0)
            keep_q(0, 0, 0)
            keep_q(0, 0, 1)
            keep_x(1, 1)

            def body(n, u):
                if has(n + 2):
                    keep_x(n + 2, u)
                if has(n - 1):
                    keep_sums_a(n - 1, 1 - u)
                if has(n + 1):
                    keep_v(n + 1, 1 - u)
                    high_parts(n + 1)
                    middle_parts(n + 1)
                    keep_k(n + 1, 1 - u)
                if has(n):
                    keep_nmax(n, u)
                if has(n + 1):
                    keep_q(n + 1, 1 - u, 0)
                if has(n):
                    exp(n, 0)
                if has(n + 1):
                    keep_q(n + 1, 1 - u, 1)
                if has(n):
                    exp(n, 1)
                for k, step in enumerate((0, NPAIR - 2)):
                    if isinstance(n, int) and n == step:
                        scale_weights(k)
            steps(act, body)

            def exp2(n, r, ht):
                wait(act, "t2_ready", 4 * n + ht + 1)
                wait(act, "pv2_done", 2 * (n - 1) + ht // 2 + 1)
                b = 2 * (ht % 2)
                nc.scalar.activation(probs2[:, ht].rearrange("p h l q -> p (h l q)"),
                                     ps_t[:, b:b + 2, :].rearrange("p a b -> p (a b)"), ACT.Exp, scale=SCALE).then_inc(s("exp2_done"), 1)

            def keep_maxima(n, r):
                wait(act, "mt2_ps", n + 1)
                nc.scalar.copy(nmax2_t[:, r % 2].rearrange("p g q -> p (g q)"), ps_a[0:16, 1, 0:P].bitcast(BF16)).then_inc(s("mt2_ready"), 1)

            def keep_sums(n):
                wait(act, "pv2_done", 2 * n)
                wait(act, "nd2_ready", n - 1)
                for b in range(2):
                    nc.scalar.copy(u2_sb[:, b, :], ps_a[:, 0, E * b:E * b + E]).then_inc(s("us2_ready"), 1)

            keep_maxima(0, 0)

            def body2(n, r):
                known = isinstance(n, int)
                exp2(n, r, 0)
                if not known or n + 1 < B:
                    keep_maxima(n + 1, (r + 1) % 4)
                if r % 2 == 0 and (not known or n > 0):
                    keep_sums(n)
                exp2(n, r, 1)
                exp2(n, r, 2)
                exp2(n, r, 3)
            steps2(act, body2)
            keep_sums(B)

            for half in range(2):
                cols = xb[:, 4 * half:4 * half + 4].rearrange("p n d -> p (n d)")
                act.wait_ge(s("inv_ready"), 3)
                nc.scalar.activation(cols, cols, ACT.Copy, scale=inv[:, 2:3]).then_inc(s("xs_ready"), 1)

            def turned(half):
                act.wait_ge(s("x8t_ps"), half + 1)
                for k in range(KT):
                    nc.scalar.copy(x8_t[:, k, 512 * half:512 * half + 512], x8_ps(half, k)).then_inc(s("x8t_ready"), 1)

            turned(0)
            turned(1)
            for i in range(2 * FT):
                half, f = i // FT, i % FT
                part = hid[:, f, 512 * half:512 * half + 512]
                act.wait_ge(s("relu_ready"), i + 1)
                nc.scalar.activation(part, part, ACT.Square, scale=step1[:, 0:1]).then_inc(s("hid_ready"), 1)
            act.wait_ge(s("bias_ps"), 1)
            act.wait_ge(s("step2_ready"), 1)
            nc.scalar.activation(y2[:], ps_a[:, 0, 0:E], ACT.Copy, scale=step2[:, 0:1]).then_inc(s("bias_ready"), 1)

        @block.vector
        def _(dve):
            NQ = QKV - H * D
            def heads_of(ap):
                return ap.rearrange("p (h d) -> p h d", d=D)

            def norm_a(first, end):
                for n in range(first, end):
                    nc.vector.bn_stats(stats[:, n, :], x_in[:, n, :]).then_inc(s("chain_a"), 1)
                dve.wait_ge(s("chain_a"), 2 * first + end - first)
                for n in range(first, end):
                    nc.vector.bn_aggr(mv[:, n, :], stats[:, n, :]).then_inc(s("chain_a"), 1)
                dve.wait_ge(s("chain_a"), 2 * end)
                nc.vector.tensor_scalar(var[:, first:end], mv[:, first:end, 1], EPS, None, ALU.add).then_inc(s("var_ready"), 1)

            def apply_a(n, u):
                known = isinstance(n, int)
                if known:
                    dve.wait_ge(s("rstd_ready"), 1 if n < 2 else 2)
                wait(dve, "xt_ps", n - 1)
                mean = mv[:].rearrange("p n d -> p (n d)")
                mean = mean[:, 2 * n:2 * n + 1] if known else mean[:, bass.ds(2 * n, 1)]
                nc.vector.tensor_scalar(xn[:, u, :] if known else xn[:, u:u + 1, :], at(x_in, n), mean,
                                        rstd[:, n:n + 1] if known else rstd[:, bass.ds(n, 1)],
                                        ALU.subtract, ALU.mult).then_inc(s("xn_ready"), 1)

            def rotate(n, u):
                wait(dve, "proj_ready", n + 1)
                heads = bank[1][:, 0:NQ].rearrange("p (a d) -> p a d", d=D)
                sh = rope_s[:].rearrange("p (a d) -> p a d", d=D)
                nc.vector.tensor_tensor(rope_c[:].rearrange("p (a d) -> p a d", d=D), heads,
                                        const[:, C_COS:C_COS + D].unsqueeze(1).to_broadcast([P, NQ // D, D]), ALU.mult).then_inc(s("chain_rope"), 1)
                nc.vector.tensor_tensor(sh[:, :, 0:4], heads[:, :, 4:8],
                                        const[:, C_SIN:C_SIN + 4].unsqueeze(1).to_broadcast([P, NQ // D, 4]), ALU.mult).then_inc(s("chain_rope"), 1)
                nc.vector.tensor_tensor(sh[:, :, 4:8], heads[:, :, 0:4],
                                        const[:, C_SIN + 4:C_SIN + 8].unsqueeze(1).to_broadcast([P, NQ // D, 4]), ALU.mult).then_inc(s("chain_rope"), 1)
                wait(dve, "chain_rope", 3 * n + 3)
                wait(dve, "qt_ps", 2 * n)
                nc.vector.tensor_tensor(split_qk[:, :, 0:D], heads_of(rope_c[:]), heads_of(rope_s[:]), ALU.add).then_inc(s("hi_ready"), 1)
                nc.vector.tensor_tensor(qk[:, u, :], rope_c[:], rope_s[:], ALU.add).then_inc(s("qk_ready"), 1)

            def parts_of_qk(n, u):
                link = chained(dve, "chain_rest", n, 1)
                wait(dve, "qk_ready", n + 1)
                link(nc.vector.tensor_tensor(heads_of(rest_qk[:]), heads_of(qk[:, u]), split_qk[:, :, 0:D], ALU.subtract))
                nc.vector.tensor_copy(split_qk[:, :, 4 * D:5 * D], heads_of(rest_qk[:])).then_inc(s("mid_ready"), 1)

            def low_parts(n):
                wait(dve, "mid_ready", n + 1)
                for first, end, place in ((0, G * H, 5), (G * H, NH, 2)):
                    ins = nc.vector.tensor_tensor(split_qk[:, first:end, D * place:D * place + D], heads_of(rest_qk[:])[:, first:end],
                                                  split_qk[:, first:end, 4 * D:5 * D], ALU.subtract)
                ins.then_inc(s("lo_ready"), 1)

            def maxima_a(n, u, which):
                for k in which:
                    b, gp = k // 2, k % 2
                    wait(dve, "s_ready", 4 * n + k + 1)
                    nc.vector.tensor_reduce(nmax[:, u, gp, :, b], ps_t[:, 2 + k % 2, :].rearrange("p (h t) -> p h t", t=T), AX.X, ALU.max,
                                            negate=True).then_inc(s("max_done"), 1)

            def split_maxima_a(n, u):
                link = chained(dve, "chain_max", n, 1)
                wait(dve, "max_done", 4 * n + 4)
                flat = nmax[:, u].rearrange("p g h b -> p g (h b)")
                link(nc.vector.tensor_copy(nmax_p[:, u, :, 0, :], flat))
                nc.vector.tensor_tensor(nmax_p[:, u, :, 1, :], flat, nmax_p[:, u, :, 0, :], ALU.subtract).then_inc(s("nmax_ready"), 1)

            def invert(n):
                wait(dve, "nd_ready", n + 1)
                nc.vector.reciprocal(rden[:], ps_a[:, 1, 0:E]).then_inc(s("inverted"), 1)

            def divide(n, u):
                wait(dve, "inverted", n + 1)
                nc.vector.tensor_tensor(y_t[:, u, :], ps_a[:, 1, E:2 * E], rden[:], ALU.mult).then_inc(s("y_ready"), 1)

            def norm_c(n):
                link = chained(dve, "chain_norm", n, 2)
                wait(dve, "w_ready", n + 1)
                x1_n = at(x1, n)
                nc.vector.tensor_tensor(x1_n, out_ps(n) if isinstance(n, int) else out_ps(n).unsqueeze(1), at(xb, n), ALU.add
                                        ).then_inc(s("x1_ready"), 1)
                wait(dve, "x1_ready", n + 1, alone=True)
                link(nc.vector.bn_stats(stats2[:], x1_n), alone=True)
                link(nc.vector.bn_aggr(mv2[:], stats2[:]))
                nc.vector.tensor_scalar(var2[:], mv2[:, 1:2], EPS, None, ALU.add).then_inc(s("var2_ready"), 1)

            def apply_c(n, u):
                wait(dve, "rstd2_ready", n + 1)
                nc.vector.tensor_scalar(x1n[:, u, :] if isinstance(n, int) else x1n[:, u:u + 1, :], at(x1, n), mv2[:, 0:1], rstd2[:],
                                        ALU.subtract, ALU.mult).then_inc(s("x1n_ready"), 1)

            def maxima(n, r, ht):
                for hp in range(2):
                    wait(dve, "s2_ready", 8 * n + 2 * ht + hp + 1)
                    nc.vector.tensor_reduce(nmax2[:, r % 2, :, hp, ht], bank[hp][:].rearrange("p (a k) -> p a k", k=E), AX.X, ALU.max,
                                            negate=True).then_inc(s("max2_done"), 1)

            def split_maxima(n, r):
                link = chained(dve, "chain_max2", n, 1)
                wait(dve, "max2_done", 8 * n + 8)
                wait(dve, "mt2_ps", n - 1)
                link(nc.vector.tensor_copy(nmax2_p[:, r % 2, :, :, 0, :], nmax2[:, r % 2]))
                nc.vector.tensor_tensor(nmax2_p[:, r % 2, :, :, 1, :], nmax2[:, r % 2], nmax2_p[:, r % 2, :, :, 0, :],
                                        ALU.subtract).then_inc(s("nmax2_ready"), 1)

            link_w = chained(dve, "chain_round", 0, 100)

            def scale_of(k):
                dve.wait_ge(s("top_all_ready"), k + 1)
                link_w(nc.vector.tensor_scalar(unit[:, k:k + 1], top_all[:, k:k + 1], 1.0 / FP8_MAX, 1e-6, ALU.mult, ALU.max))
                link_w(nc.vector.reciprocal(inv[:, k:k + 1], unit[:, k:k + 1]))
                dve.sem_inc(s("inv_ready"), 1)

            def magic_of(src, cols):
                m = magic[:, cols]
                link_w(nc.vector.tensor_scalar(m.bitcast(U32), src.bitcast(U32), 0x7F800000, None, ALU.bitwise_and))
                link_w(nc.vector.tensor_scalar(m, m, 2.0 ** -6, 1.5 * 2.0 ** 20, ALU.max, ALU.mult))

            w_flat = [w[:].rearrange("p k n -> p (k n)") for w in (wf, wp)]
            w8_flat = [w.rearrange("p k n -> p (k n)") for w in (wf8[:], wp8[:, 0])]
            every = slice(0, NPAIR * E)

            def top_of_weights(k):
                dve.wait_ge(s("ld_ffn"), 32)
                nc.vector.tensor_reduce(top[:, k:k + 1], w_flat[k], AX.X, ALU.max, apply_absolute_value=True
                                        ).then_inc(s("top_ready"), 1)

            def magic_of_weights(k):
                dve.wait_ge(s("ws_ready"), k + 1)
                magic_of(w_flat[k], every)

            def add_magic(k):
                link_w(nc.vector.tensor_tensor(w_flat[k], w_flat[k], magic[:], ALU.add))

            def round_weights(k):
                link_w(nc.vector.tensor_tensor(w8_flat[k], w_flat[k], magic[:], ALU.subtract))

            dve.wait_ge(s("ld_bias"), 16)
            link = chained(dve, "chain_bias", 0, 3)
            link(nc.vector.tensor_copy(b_parts[:, 0], b_qkv[:]))
            link(nc.vector.tensor_tensor(b_rest[:], b_qkv[:], b_parts[:, 0], ALU.subtract))
            link(nc.vector.tensor_copy(b_parts[:, 1], b_rest[:]))
            nc.vector.tensor_tensor(b_parts[:, 2], b_rest[:], b_parts[:, 1], ALU.subtract).then_inc(s("bias_parts"), 1)
            dve.wait_ge(s("ld_x"), 16)
            norm_a(0, 2)
            apply_a(0, 0)
            apply_a(1, 1)
            nc.vector.memset(split_qk[:].rearrange("p h c -> p (h c)").bitcast(F32), 0.0).then_inc(s("setup_dve"), 1)
            nc.vector.memset(k_z[:].rearrange("p u h a t -> p (u h a t)").bitcast(F32), 0.0).then_inc(s("setup_dve"), 1)
            dve.wait_ge(s("ld_const"), 16)
            rotate(0, 0)
            parts_of_qk(0, 0)
            low_parts(0)
            dve.wait_ge(s("ld_xr"), 16)
            norm_a(2, NPAIR)

            def body(n, u):
                known = isinstance(n, int)
                last = known and n == NPAIR
                if has(n + 2):
                    apply_a(n + 2, u)
                if has(n + 1):
                    rotate(n + 1, 1 - u)
                if has(n - 2):
                    norm_c(n - 2)
                if has(n):
                    maxima_a(n, u, (0,))
                if last:
                    maxima(0, 0, 0)
                    maxima(0, 0, 1)
                if has(n):
                    maxima_a(n, u, (1,))
                if has(n + 1):
                    parts_of_qk(n + 1, 1 - u)
                if has(n):
                    maxima_a(n, u, (2,))
                if has(n + 1):
                    low_parts(n + 1)
                if has(n - 2):
                    apply_c(n - 2, u)
                if has(n):
                    maxima_a(n, u, (3,))
                    split_maxima_a(n, u)
                if has(n - 1):
                    invert(n - 1)
                    divide(n - 1, 1 - u)
                if last:
                    dve.sem_inc(s("nd2_read"), 1)
                    maxima(0, 0, 2)
                    maxima(0, 0, 3)
                    split_maxima(0, 0)
                if known and n == 0:
                    top_of_weights(0)
                    top_of_weights(1)
                if known and n == 1:
                    magic_of_weights(0)
                if known and n == NPAIR - 2:
                    add_magic(0)
                if known and n == NPAIR - 1:
                    round_weights(0)
                    dve.sem_inc(s("wf8_ready"), 1)
                if last:
                    norm_c(n - 1)
                if last:
                    apply_c(n - 1, 1 - u)
                if known and n == 0:
                    for k in range(2):
                        scale_of(k)
            steps(dve, body)

            def finish(n):
                known = isinstance(n, int)
                cols = slice(P * (n - 2), P * n) if known else bass.ds(P * (n - 2), 2 * P)
                flat = [a[:].rearrange("p n d -> p (n d)")[:, cols] for a in (x1, x2)]
                wait(dve, "nd2_ready", n + 1)
                nc.vector.reciprocal(rden2[:], ps_a[:, 1, E:2 * E]).then_inc(s("nd2_read"), 1)
                wait(dve, "nd2_read", n)
                nc.vector.tensor_tensor(y2[:], ps_a[:, 1, 0:E], rden2[:], ALU.mult).then_inc(s("nd2_read"), 1)
                wait(dve, "nd2_read", n + 1)
                nc.vector.scalar_tensor_tensor(out=flat[1], in0=y2[:], scalar=gam[:, 0:1], in1=flat[0], op0=ALU.mult, op1=ALU.add
                                               ).then_inc(s("x2_ready"), 2)

            def moments(n, stage):
                known = isinstance(n, int)
                if stage == 0:
                    cols = slice(P * (n - 2), P * n) if known else bass.ds(P * (n - 2), 2 * P)
                    wait(dve, "x2_ready", n, alone=True)
                    nc.vector.bn_stats(stats3[:], x2[:].rearrange("p n d -> p (n d)")[:, cols]).then_inc(s("stat3_ready"), 2)
                if stage == 1:
                    wait(dve, "stat3_ready", n, alone=True)
                    wait(dve, "x3_ready", n - 1, alone=True)
                    nc.vector.bn_aggr(mv3[:], stats3[:]).then_inc(s("mv3_ready"), 2)
                if stage == 2:
                    wait(dve, "mv3_ready", n)
                    nc.vector.tensor_scalar(var3[:], mv3[:, 1:2], EPS, None, ALU.add).then_inc(s("var3_ready"), 2)

            def top_of_x(first, end):
                dve.wait_ge(s("x3_ready"), 2 * end + 1)
                nc.vector.tensor_reduce(top_x[:, first:end], xb[:, first:end], AX.X, ALU.max, apply_absolute_value=True
                                        ).then_inc(s("topx_ready"), end - first)

            for ht in range(4):
                maxima(1, 1, ht)
            split_maxima(1, 1)

            def body2(n, r):
                known = isinstance(n, int)
                ahead = not known or n + 2 < B
                if ahead:
                    for ht in range(3):
                        maxima(n + 2, (r + 2) % 4, ht)
                if r % 2 == 0 and (not known or n > 0):
                    finish(n)
                if ahead:
                    maxima(n + 2, (r + 2) % 4, 3)
                done = r % 2 == 0 and (not known or n > 0)
                if done:
                    moments(n, 0)
                if ahead:
                    split_maxima(n + 2, (r + 2) % 4)
                if done:
                    moments(n, 1)
                    moments(n, 2)
                if known and n == B - 2:
                    magic_of_weights(1)
                    add_magic(1)
                    top_of_x(0, NPAIR - 2)
                if known and n == B - 1:
                    top_of_x(NPAIR - 2, NPAIR - 1)
            steps2(dve, body2)
            finish(B)
            for k in range(3):
                moments(B, k)
            round_weights(1)
            dve.sem_inc(s("wp8_ready"), 1)
            top_of_x(NPAIR - 1, NPAIR)

            link = chained(dve, "chain_ffn", 0, 100)
            dve.wait_ge(s("topx_ready"), NPAIR)
            nc.vector.tensor_reduce(top[:, 2:3], top_x[:], AX.X, ALU.max).then_inc(s("top_ready"), 1)
            scale_of(2)
            link(nc.vector.tensor_tensor(step1[:], unit[:, 0:1], unit[:, 2:3], ALU.mult))
            xn_all = xb[:].rearrange("p n d -> p (n d)")
            x8_all = x8.rearrange("p n d -> p (n d)")
            for half in range(2):
                cols = slice(1024 * half, 1024 * half + 1024)
                dve.wait_ge(s("xs_ready"), half + 1)
                magic_of(xn_all[:, cols], cols)
                link(nc.vector.tensor_tensor(xn_all[:, cols], xn_all[:, cols], magic[:, cols], ALU.add))
                nc.vector.tensor_tensor(x8_all[:, cols], xn_all[:, cols], magic[:, cols], ALU.subtract).then_inc(s("x8_ready"), 1)
            for i in range(2 * FT):
                half, f = i // FT, i % FT
                dve.wait_ge(s("fc1_ready"), i + 1)
                nc.vector.tensor_scalar(hid[:, f, 512 * half:512 * half + 512], ps_t[:, i % 4, :], 0.0, None, ALU.max, ALU.max,
                                        accum_out=tops[:, i:i + 1]).then_inc(s("relu_ready"), 1)
            dve.wait_ge(s("relu_ready"), 2 * FT)
            link(nc.vector.tensor_reduce(top[:, 3:4], tops[:], AX.X, ALU.max))
            link(nc.vector.tensor_tensor(top[:, 3:4], top[:, 3:4], step1[:], ALU.mult))
            nc.vector.tensor_tensor(top[:, 3:4], top[:, 3:4], top[:, 3:4], ALU.mult).then_inc(s("top_ready"), 1)
            scale_of(3)
            link(nc.vector.tensor_scalar(half_inv[:], inv[:, 3:4], 0.5, None, ALU.mult))
            nc.vector.tensor_tensor(step2[:], unit[:, 1:2], unit[:, 3:4], ALU.mult).then_inc(s("step2_ready"), 1)
            for first, end in H_CHUNKS:
                c = slice(P * first, P * end)
                dve.wait_ge(s("hid_ready"), FT * (first // 4 + 1))
                nc.vector.tensor_scalar(h_lo[:, :, c], hid[:, :, c], inv[:, 3:4], TINY, ALU.mult, ALU.min, saturate=False
                                        ).then_inc(s("hq_ready"), 1)
                nc.vector.tensor_scalar(h_hi[:, :, c], hid[:, :, c], half_inv[:], TINY / 2, ALU.mult, ALU.max, saturate=False
                                        ).then_inc(s("hq_ready"), 1)
            dve.wait_ge(s("base_ready"), 1)
            for n in range(NPAIR):
                dve.wait_ge(s("fc2_ready"), n + 1)
                nc.vector.scalar_tensor_tensor(out=res[:, n, :], in0=fc2_ps[n], scalar=step2[:, 0:1], in1=xb[:, n, :],
                                               op0=ALU.mult, op1=ALU.add).then_inc(s("res_ready"), 1)


def constants():
    import numpy as np
    f = np.float32
    c = np.zeros((P, C_END), f)
    j = np.arange(D // 2, dtype=f)
    theta = f(10000.0) ** (f(-2.0) * j / f(D))
    ang = (np.arange(T, dtype=f) + f(1.0))[:, None] * theta[None, :].astype(f)
    ang = np.concatenate([ang, ang], -1)
    c[:, C_COS:C_COS + D] = np.tile(np.cos(ang), (2, 1))
    sin = np.sin(ang)
    sin[:, :D // 2] *= -1
    c[:, C_SIN:C_SIN + D] = np.tile(sin, (2, 1))
    c[:, C_ID:C_ID + P] = np.eye(P, dtype=f)
    for b in range(2):
        for h in range(H):
            for d in range(D):
                row, col = 32 * (h % 4) + 16 * b + d, P * (h // 4) + 64 * b + D * h + d
                c[row, C_NUM + col] = 1.0
                c[row + D, C_DEN + col] = 1.0
    for h in range(H):
        for d in range(D):
            row = 32 * (h % 4) + 16 * (h // 4) + d
            c[row, C_NUM2 + D * h + d] = 1.0
            c[row + D, C_DEN2 + D * h + d] = 1.0
    one = 0x3F80
    low = np.array([-1e30], f).view(np.uint32)[0] >> 16
    t = np.arange(T)
    mask = np.where(t[None, :] > t[:, None], low, 0).astype(np.uint16)
    tokens = one * np.eye(T, dtype=np.uint16)
    cb = np.zeros((P, B_END), np.uint16)
    cb[:, B_ID:B_ID + P] = one * np.eye(P, dtype=np.uint16)
    for j2 in range(16):
        for part in range(2):
            cb[16 * part + j2, B_HEAD + T * j2:B_HEAD + T * j2 + T] = one
        cb[64:, B_HEAD + T * j2:B_HEAD + T * j2 + T] = mask
    cb[:T, B_TOKEN:B_TOKEN + P] = np.tile(tokens, (1, 2))
    cb[:T, B_MASK:B_MASK + H * T] = np.tile(mask, (1, H))
    cb[64:, B_NMAX:] = np.tile(tokens, (1, 8))
    ck = np.zeros((2, 2, 4, 2, 4 * E), np.uint16)
    for hp in range(2):
        ck[hp, :, :, hp] = one
    return c, cb, ck.reshape(4, -1)


def kernel(x, ctx_2048, L0_attn_Wq, L0_attn_bq, L0_attn_Wk, L0_attn_bk, L0_attn_Wv, L0_attn_bv, L0_attn_Wo,
           L0_attn_bo, L0_xattn_gamma, L0_ffn_w_fc, L0_ffn_w_proj):
    import numpy as np
    import concourse.bacc as bacc
    from concourse.bass_utils import run_bass_kernel_spmd
    x, ctx, wq, bq, wk, bk, wv, bv, wo, bo, gamma, wfc, wproj = (np.asarray(a) for a in (
        x, ctx_2048, L0_attn_Wq, L0_attn_bq, L0_attn_Wk, L0_attn_bk, L0_attn_Wv, L0_attn_bv, L0_attn_Wo, L0_attn_bo,
        L0_xattn_gamma, L0_ffn_w_fc, L0_ffn_w_proj))
    wq = wq.reshape(H, G, D, E).transpose(1, 0, 2, 3).reshape(E, E)
    bq = bq.reshape(H, G, D).transpose(1, 0, 2).reshape(E)
    cf, cb, ck = constants()
    arrays = {
        "x": x.reshape(B * T, E),
        "ctxt": ctx.reshape(B * T, E),
        "ctxt_t": ctx.reshape(B * T, E).T,
        "wqkv": np.concatenate([wq, wk, wv]).T,
        "bqkv": np.concatenate([bq, bk, bv])[None],
        "wo": wo.reshape(E, H, 2, 2, D).transpose(3, 1, 4, 2, 0).reshape(2 * H * D, 2, E),
        "bo": bo,
        "gamma": gamma.reshape(1),
        "wfc": wfc.T,
        "wproj": wproj.T,
        "cf": cf,
        "cb": cb,
        "ck": ck,
    }
    nc = bacc.Bacc("TRN2", target_bir_lowering=False, num_devices=1)
    ins, args = {}, {}
    for name, a in arrays.items():
        a = np.ascontiguousarray(a)
        ins[f"in_{name}"] = a
        args[name] = nc.dram_tensor(f"in_{name}", a.shape, mybir.dt.from_np(a.dtype), kind="ExternalInput").ap()
    out = nc.dram_tensor("out_x", (B * T, E), F32, kind="ExternalOutput").ap()
    build(nc, **args, out=out)
    r = run_bass_kernel_spmd(nc, [ins], core_ids=[0])
    return r.results[0]["out_x"].reshape(B, T, E)
```
